# Optimizing a Trainium2 kernel written in Bass

```python
import numpy as np
import jax
import jax.numpy as jnp

def _softmax(x, axis=-1):
    return jax.nn.softmax(x, axis=axis)

def _gelu(x):
    return jax.nn.gelu(x, approximate=True)

def _silu(x):
    return jax.nn.silu(x)

def _sigmoid(x):
    return jax.nn.sigmoid(x)

def _layernorm(x, axis=-1, eps=1e-05):
    m = jnp.mean(x, axis=axis, keepdims=True)
    v = jnp.var(x, axis=axis, keepdims=True)
    return (x - m) / jnp.sqrt(v + eps)

def _scatter_add(tgt, idx, src, axis=0):
    return tgt.at[idx].add(src)

def _segment_sum(src, seg, n):
    return jax.ops.segment_sum(src, seg, n)
kernel_name = 'mk_flamingo_gated_d1_seqx_r4_0cde8a'

def setup_inputs(seed: int=0):
    np.random.seed(seed)
    _w = jnp.asarray

    def _rec_inputs():
        import jax
        import jax.numpy as jnp
        _rk = jax.random.key(seed)
        x = -0.0002928 + 1 * jax.random.normal(jax.random.fold_in(_rk, 1), (4, 1024, 256), jnp.float32)
        _lenS = 1024 - jax.random.randint(jax.random.fold_in(_rk, 7), (4,), 0, max(1, 1024 // 4) + 1, jnp.int32)
        _lenS2 = 64 - jax.random.randint(jax.random.fold_in(_rk, 8), (4,), 0, max(1, 64 // 4) + 1, jnp.int32)
        _ctx_1024P = jax.random.normal(jax.random.fold_in(_rk, 11), (4, 16, 256), jnp.float32)
        _ctx_1024c = jax.random.dirichlet(jax.random.fold_in(_rk, 511), 0.3 * jnp.ones((16,), jnp.float32), (4, 64))
        _ctx_1024t = jnp.einsum('bsk,bkd->bsd', _ctx_1024c, _ctx_1024P)
        _ctx_1024t = _ctx_1024t * jax.lax.rsqrt(jnp.mean(jnp.square(_ctx_1024t)) + 1e-12) * 0.953939
        ctx_1024 = -1.39393e-06 + 0.999914 * (_ctx_1024t + 0.3 * jax.random.normal(jax.random.fold_in(_rk, 611), (4, 64, 256), jnp.float32))
        _validS = jnp.arange(1024)[None, :] < _lenS[:, None]
        _validS2 = jnp.arange(64)[None, :] < _lenS2[:, None]
        _causal = jnp.tril(jnp.ones((1024, 1024), dtype=bool))
        mask_1xS2_if1 = jnp.where(jnp.ones((1, 64), dtype=bool), 1, 0).astype(jnp.int32)
        _g = jax.random.normal(jax.random.fold_in(_rk, 9001), (2, 1), jnp.float32)
        _g = jnp.sign(_g) * jnp.maximum(jnp.abs(_g), 1.0) + (_g == 0) * 1.0
        g_xattn = _g[0]
        g_ffn = _g[1]
        return (x, ctx_1024, mask_1xS2_if1, g_xattn, g_ffn)
    x, ctx_1024, mask_1xS2_if1, g_xattn, g_ffn = _rec_inputs()

    def _L0_xattn_setup():
        import jax, jax.numpy as jnp
        import numpy as np
        D_MODEL = 256
        N_HEADS = 16
        HEAD_DIM = D_MODEL // N_HEADS
        key = jax.random.key(seed)
        ks = jax.random.split(key, 12)
        B, S = (1, 1024)
        s = 1.0 / np.sqrt(D_MODEL)
        return {'query': jax.random.normal(ks[0], (B, S, D_MODEL), jnp.float32), 'key': jax.random.normal(ks[1], (B, S, D_MODEL), jnp.float32), 'value': jax.random.normal(ks[2], (B, S, D_MODEL), jnp.float32), 'attention_mask': jnp.ones((B, S), jnp.int32), 'Wq': jax.random.normal(ks[3], (D_MODEL, D_MODEL), jnp.float32) * s, 'bq': jax.random.normal(ks[4], (D_MODEL,), jnp.float32) * s, 'Wk': jax.random.normal(ks[5], (D_MODEL, D_MODEL), jnp.float32) * s, 'bk': jax.random.normal(ks[6], (D_MODEL,), jnp.float32) * s, 'Wv': jax.random.normal(ks[7], (D_MODEL, D_MODEL), jnp.float32) * s, 'bv': jax.random.normal(ks[8], (D_MODEL,), jnp.float32) * s, 'Wo': jax.random.normal(ks[9], (D_MODEL, D_MODEL), jnp.float32) * s, 'bo': jax.random.normal(ks[10], (D_MODEL,), jnp.float32) * s}
    _L0_xattn_all = _L0_xattn_setup()
    _L0_xattn_in = {k: v for k, v in _L0_xattn_all.items() if k in ('Wq', 'bq', 'Wk', 'bk', 'Wv', 'bv', 'Wo', 'bo')}
    del _L0_xattn_all

    def _L0_ffn_setup():
        import jax, jax.numpy as jnp
        import numpy as np
        NUM_LOCAL_EXPERTS = 8
        D_MODEL = 256
        D_FF = 1024
        B, EC = (4, NUM_LOCAL_EXPERTS * 256)
        key = jax.random.key(seed)
        k_in, k_w1, k_w2 = jax.random.split(key, 3)
        s1 = 1.0 / np.sqrt(D_MODEL)
        s2 = 1.0 / np.sqrt(D_FF)
        return {'inputs': jax.random.normal(k_in, (B, EC, D_MODEL), dtype=jnp.float32), 'w1': jax.random.normal(k_w1, (NUM_LOCAL_EXPERTS, D_FF, D_MODEL), dtype=jnp.float32) * s1, 'b1': jnp.zeros((NUM_LOCAL_EXPERTS, D_FF), dtype=jnp.float32), 'w2': jax.random.normal(k_w2, (NUM_LOCAL_EXPERTS, D_MODEL, D_FF), dtype=jnp.float32) * s2, 'b2': jnp.zeros((NUM_LOCAL_EXPERTS, D_MODEL), dtype=jnp.float32)}
    _L0_ffn_all = _L0_ffn_setup()
    _L0_ffn_in = {k: v for k, v in _L0_ffn_all.items() if k in ('w1', 'b1', 'w2', 'b2')}
    del _L0_ffn_all
    return {'x': x, 'ctx_1024': ctx_1024, 'mask_1xS2_if1': mask_1xS2_if1, 'g_xattn': g_xattn, 'g_ffn': g_ffn, 'L0_xattn_Wq': _L0_xattn_in['Wq'], 'L0_xattn_bq': _L0_xattn_in['bq'], 'L0_xattn_Wk': _L0_xattn_in['Wk'], 'L0_xattn_bk': _L0_xattn_in['bk'], 'L0_xattn_Wv': _L0_xattn_in['Wv'], 'L0_xattn_bv': _L0_xattn_in['bv'], 'L0_xattn_Wo': _L0_xattn_in['Wo'], 'L0_xattn_bo': _L0_xattn_in['bo'], 'L0_ffn_w1': _L0_ffn_in['w1'], 'L0_ffn_b1': _L0_ffn_in['b1'], 'L0_ffn_w2': _L0_ffn_in['w2'], 'L0_ffn_b2': _L0_ffn_in['b2']}

def reference(x, ctx_1024, mask_1xS2_if1, g_xattn, g_ffn, L0_xattn_Wq, L0_xattn_bq, L0_xattn_Wk, L0_xattn_bk, L0_xattn_Wv, L0_xattn_bv, L0_xattn_Wo, L0_xattn_bo, L0_ffn_w1, L0_ffn_b1, L0_ffn_w2, L0_ffn_b2):
    import jax
    import jax.numpy as jnp

    def _L0_xattn_ref(query, key, value, attention_mask, Wq, bq, Wk, bk, Wv, bv, Wo, bo):
        import jax, jax.numpy as jnp
        import numpy as np
        D_MODEL = 256
        N_HEADS = 16
        HEAD_DIM = D_MODEL // N_HEADS
        B = query.shape[0]

        def split_heads(x):
            return x.reshape(B, -1, N_HEADS, HEAD_DIM).transpose(0, 2, 1, 3)
        q = split_heads(query @ Wq + bq)
        k = split_heads(key @ Wk + bk)
        v = split_heads(value @ Wv + bv)
        scores = jnp.einsum('bhqd,bhkd->bhqk', q, k) / np.sqrt(HEAD_DIM)
        mask = attention_mask[:, None, None, :]
        scores = jnp.where(mask == 0, jnp.float32(-1000000000.0), scores)
        weights = jax.nn.softmax(scores, axis=-1)
        out = jnp.einsum('bhqk,bhkd->bhqd', weights, v)
        out = out.transpose(0, 2, 1, 3).reshape(B, -1, D_MODEL)
        return out @ Wo + bo

    def _L0_ffn_ref(inputs, w1, b1, w2, b2):
        import jax, jax.numpy as jnp
        import numpy as np
        NUM_LOCAL_EXPERTS = 8
        D_MODEL = 256
        D_FF = 1024
        B, EC = (4, NUM_LOCAL_EXPERTS * 256)
        B_, EC_, D = inputs.shape
        E = w1.shape[0]
        C = EC_ // E
        x = inputs.reshape(B_, E, C, D)
        h = jnp.einsum('becd,efd->becf', x, w1) + b1[None, :, None, :]
        h = jax.nn.gelu(h, approximate=False)
        y = jnp.einsum('becf,edf->becd', h, w2) + b2[None, :, None, :]
        return y.reshape(B_, EC_, D)
    x = x + jnp.tanh(g_xattn[0]) * _L0_xattn_ref(_layernorm(x, axis=-1), ctx_1024, ctx_1024, mask_1xS2_if1, L0_xattn_Wq, L0_xattn_bq, L0_xattn_Wk, L0_xattn_bk, L0_xattn_Wv, L0_xattn_bv, L0_xattn_Wo, L0_xattn_bo)
    x = x + jnp.tanh(g_ffn[0]) * _L0_ffn_ref(_layernorm(x, axis=-1), L0_ffn_w1, L0_ffn_b1, L0_ffn_w2, L0_ffn_b2)
    return x

_drawn_inputs = setup_inputs


def setup_inputs(seed=0):
    import zlib

    import numpy as np

    out = dict(_drawn_inputs(seed))
    spreads = {'L0_ffn_b1': (0.0, 0.1), 'L0_ffn_b2': (0.0, 0.1)}
    factors = {'L0_xattn_bq': 5.409, 'L0_xattn_bk': 8.0}
    for name, (base, spread) in spreads.items():
        noise = np.random.default_rng([zlib.crc32(name.encode()), seed]).standard_normal(out[name].shape)
        drawn = base * np.exp(spread * noise) if base else spread * noise
        out[name] = jnp.asarray(drawn.astype(out[name].dtype))
    for name, factor in factors.items():
        out[name] = (out[name] * factor).astype(out[name].dtype)
    return out
```

```python
from contextlib import ExitStack

import concourse.bass as bass
from concourse import mybir

F32 = mybir.dt.float32
F32R = mybir.dt.float32r
I32 = mybir.dt.int32
ALU = mybir.AluOpType
ACT = mybir.ActivationFunctionType
AX_X = mybir.AxisListType.X

P = 128
D = 256
C = D // P
B = 4
S = 1024
E = S // P
TOK = B * P
F = 1024
FC = F // P
H = 16
HD = D // H
K = 64
HG = H // C
PAIRS = H // 2
PW = 2 * HD + 2
PVN = 96
EPS = 1e-5
SCALE = 0.25


def build(nc, x, ctx, mask, g_x, g_f, wq, bq, wk, bk, wv, bv, wo, bo, w1, b1, w2, b2, out):
    stack = ExitStack()
    with stack:
        def sb(name, shape, dt=F32):
            return stack.enter_context(nc.sbuf_tensor(name, shape, dt))

        def sem(name):
            return stack.enter_context(nc.semaphore(name))

        xs = sb("xs", [P, E * B * D])
        attn = sb("attn", [P, B, D])
        norm = sb("norm", [P, B, D])
        xT_hi = sb("xT_hi", [P, C, TOK], F32R)
        xT_lo = sb("xT_lo", [P, C, TOK], F32R)
        fT_hi = sb("fT_hi", [P, C, TOK], F32R)
        fT_lo = sb("fT_lo", [P, C, TOK], F32R)
        qT_hi = sb("qT_hi", [P, C, TOK], F32R)
        qT_lo = sb("qT_lo", [P, C, TOK], F32R)
        oT_hi, oT_lo = qT_hi, qT_lo
        prob = sb("prob", [P, 2, H * K])
        probT = sb("probT", [P, 2, PAIRS, P])
        hid = sb("hid", [P, 2, TOK])
        hT_hi = sb("hT_hi", [P, FC, TOK], F32R)
        hT_lo = sb("hT_lo", [P, FC, TOK], F32R)
        w_raw = sb("w_raw", [P, C * F])
        w1_hi = sb("w1_hi", [P, C, F], F32R)
        w1_lo = sb("w1_lo", [P, C, F], F32R)
        w2_hi = sb("w2_hi", [P, FC, D], F32R)
        w2_lo = sb("w2_lo", [P, FC, D], F32R)
        wq_hi = sb("wq_hi", [P, C, D], F32R)
        wq_lo = sb("wq_lo", [P, C, D], F32R)
        wo_hi = sb("wo_hi", [P, C, D], F32R)
        wo_lo = sb("wo_lo", [P, C, D], F32R)
        keys_hi = sb("keys_hi", [P, B, C, HG, K], F32R)
        keys_lo = sb("keys_lo", [P, B, C, HG, K], F32R)
        vals = sb("vals", [P, B, (PAIRS - 1) * PW + PVN])
        ident = sb("ident", [P, P])
        b1_sb = sb("b1_sb", [P, E, FC])
        b2_sb = sb("b2_sb", [P, D])
        b2_g = sb("b2_g", [P, D])
        bo_g = sb("bo_g", [P, D])
        bq_sb = sb("bq_sb", [P, C])
        bk_sb = sb("bk_sb", [P, C])
        gates = sb("gates", [P, 2])
        gate = sb("gate", [P, 2])
        head_of = sb("head_of", [P, HG])
        minus_half = sb("minus_half", [P, B])
        stat6 = sb("stat6", [P, B, 6])
        stat2 = sb("stat2", [P, 2, B, 2])
        var_eps = sb("var_eps", [P, 2, B])
        rstd = sb("rstd", [P, 2, B])
        smax = sb("smax", [P, 2, H])
        rden = sb("rden", [P, 2, H])
        mcol_i = sb("mcol_i", [P, 1], I32)
        mcol = sb("mcol", [P, 1])
        wcol = sb("wcol", [P, 1])
        first = sb("first", [K, 1])
        w_set = prob[:, :, :].rearrange("p a (n c d) -> p (a n) c d", n=2, c=C)
        ctx_sb = probT[0:K, 0, :, :].rearrange("p j q -> p (j q)").rearrange("p (b d) -> p b d", b=B)
        ctxT = probT[:, 1, :, :].rearrange("p j q -> p (j q)").rearrange("p (c b k) -> p c b k", c=C, b=B)
        ctxG = hid[:, 0, :].rearrange("p (c n) -> p c n", c=C)
        kT = hid[:, 1, :].rearrange("p (c b k) -> p c b k", c=C, b=B)
        bv_w = attn[:, 0, :]
        bv_sb = attn[:, 1, :]
        bo_sb = attn[:, 2, :]
        small = attn[0:K, 3, :]
        mrow = small[:, 0:K]
        gsel = small[:, K:2 * K]
        gdiag = small[:, 2 * K:3 * K]
        mrow_i = sb("mrow_i", [K, K], I32)
        tri = sb("tri", [K, K])
        ones = sb("ones", [P, P])
        ident2 = sb("ident2", [K, 2, K])

        score_ps = [stack.enter_context(nc.psum_tensor(f"score_ps{i}", [P, TOK], F32)) for i in range(2)]
        trans_ps = [stack.enter_context(nc.psum_tensor(f"trans_ps{i}", [P, TOK], F32)) for i in range(2)]
        hid_ps = [stack.enter_context(nc.psum_tensor(f"hid_ps{i}", [P, TOK], F32)) for i in range(2)]
        attn_ps = [stack.enter_context(nc.psum_tensor(f"attn_ps{i}", [P, TOK], F32)) for i in range(2)]
        y_ps = [bank[:, 0:D] for bank in hid_ps]

        x0_loaded, x_loaded, w_loaded, b2_loaded = sem("x0_loaded"), sem("x_loaded"), sem("w_loaded"), sem("b2_loaded")
        attn_w_loaded, consts_loaded, ctx_loaded = sem("attn_w_loaded"), sem("consts_loaded"), sem("ctx_loaded")
        stored = sem("stored")
        waited = sem("waited")
        pool_const, pool_self, dve_self, act_self = sem("pool_const"), sem("pool_self"), sem("dve_self"), sem("act_self")
        mask_ready, count_ps_ready, gsel_ready = sem("mask_ready"), sem("count_ps_ready"), sem("gsel_ready")
        ctx_ps_ready, ctx_sb_ready, kv_ps_ready = sem("ctx_ps_ready"), sem("ctx_sb_ready"), sem("kv_ps_ready")
        kT_ready, keys_hi_ready, keys_ready, vals_zero, vals_ready = sem("kT_ready"), sem("keys_hi_ready"), sem("keys_ready"), sem("vals_zero"), sem("vals_ready")
        gate_ready, bo_ready, wq_hi_ready, attn_w_ready = sem("gate_ready"), sem("bo_ready"), sem("wq_hi_ready"), sem("attn_w_ready")
        ln1_var, rstd1_ready, xn_ready, xb_ready = sem("ln1_var"), sem("rstd1_ready"), sem("xn_ready"), sem("xb_ready")
        xT_ps_ready, xT_hi_ready, xT_ready = sem("xT_ps_ready"), sem("xT_hi_ready"), sem("xT_ready")
        q_ps_ready, q_hi_ready, q_ready = sem("q_ps_ready"), sem("q_hi_ready"), sem("q_ready")
        s_ps_ready, shifted, p_ready = sem("s_ps_ready"), sem("shifted"), sem("p_ready")
        pT_ps_ready, pT_ready, pv_ready, o_ready = sem("pT_ps_ready"), sem("pT_ready"), sem("pv_ready"), sem("o_ready")
        oT_ps_ready, oT_hi_ready, oT_ready = sem("oT_ps_ready"), sem("oT_hi_ready"), sem("oT_ready")
        wo_ps_ready, x1_ready, ln2_var, rstd2_ready, x1n_ready, x1b_ready = sem("wo_ps_ready"), sem("x1_ready"), sem("ln2_var"), sem("rstd2_ready"), sem("x1n_ready"), sem("x1b_ready")
        fT_ps_ready, fT_hi_ready, fT_ready = sem("fT_ps_ready"), sem("fT_hi_ready"), sem("fT_ready")
        h_ps_ready, gelu_done, h_hi_ready, h_ready = sem("h_ps_ready"), sem("gelu_done"), sem("h_hi_ready"), sem("h_ready")
        y_ps_ready, final_done, w_split = sem("y_ps_ready"), sem("final_done"), sem("w_split")

        def group(g, n=1):
            return xs[:, bass.ds(g * (B * D), B * D)].rearrange("p (b d) -> p b d", b=B)

        def alone(engine):
            engine.sem_inc(waited, 1)

        block = stack.enter_context(nc.Block())

        @block.sync
        def _(sp):
            def load_w(src, e):
                sp.dma_start(w_raw[:, :], src[bass.ds(e, 1), :, :].rearrange("e p n -> p (e n)")).then_inc(w_loaded, 16)

            def load_b2(e):
                sp.dma_start(b2_sb[:, :], b2[bass.ds(e, 1), :].to_broadcast([P, D])).then_inc(b2_loaded, 16)

            def store(e):
                sp.dma_start(out[bass.ds(e, 1), :, :].rearrange("e p n -> p (e n)"),
                             xs[:, bass.ds(e * (B * D), B * D)]).then_inc(stored, 16)

            sp.dma_start(mrow_i[:, :], mask.to_broadcast([K, K])).then_inc(ctx_loaded, 16)
            for half in range(2):
                sp.dma_start(mcol_i[half * K:(half + 1) * K, :], mask.rearrange("o k -> k o")).then_inc(ctx_loaded, 16)
            sp.dma_start(ctx_sb, ctx).then_inc(ctx_loaded, 16)
            sp.dma_start(xs[:, 0:B * D], x[0, :, :]).then_inc(x0_loaded, 16)
            for n, w in enumerate((wk, wv, wq, wo)):
                sp.dma_start(w_set[:, n, :, :], w).then_inc(attn_w_loaded, 16)
            sp.dma_start(bk_sb[:, :], bk).then_inc(consts_loaded, 16)
            sp.dma_start(bv_sb, bv.to_broadcast([P, D])).then_inc(consts_loaded, 16)
            sp.dma_start(bq_sb[:, :], bq).then_inc(consts_loaded, 16)
            sp.dma_start(bo_sb, bo.to_broadcast([P, D])).then_inc(consts_loaded, 16)
            sp.dma_start(gates[:, 0:1], g_x.to_broadcast([P, 1])).then_inc(consts_loaded, 16)
            sp.dma_start(gates[:, 1:2], g_f.to_broadcast([P, 1])).then_inc(consts_loaded, 16)
            sp.dma_start(b1_sb[:, :, :], b1).then_inc(consts_loaded, 16)
            load_w(w1, 0)
            load_b2(0)
            sp.dma_start(xs[:, B * D:E * B * D].rearrange("p (e n) -> p e n", e=E - 1),
                         x[1:E, :, :].rearrange("e p n -> p e n")).then_inc(x_loaded, 16)
            sp.wait_ge(w_split, 1)
            load_w(w2, 0)
            with sp.Fori(0, E - 1) as i:
                sp.wait_ge(w_split, i * 2 + 2)
                load_w(w1, i + 1)
                sp.wait_ge(x1b_ready, i + 1)
                load_b2(i + 1)
                sp.wait_ge(w_split, i * 2 + 3)
                load_w(w2, i + 1)
                sp.wait_ge(final_done, i * B + 2 * B)
                store(i)
            sp.wait_ge(final_done, E * B + B)
            store(E - 1)
            sp.wait_ge(stored, E * 16)

        @block.gpsimd
        def _(pool):
            self_count = [0]

            def done(ins):
                self_count[0] += 1
                ins.then_inc(pool_self, 1)
                pool.wait_ge(pool_self, self_count[0])

            gp = nc.gpsimd
            done(gp.memset(ident[:, :], 0.0))
            gp.affine_select(out=ident[:, :], in_=ident[:, :], compare_op=ALU.not_equal, fill=1.0, base=0,
                             pattern=[[-1, P]], channel_multiplier=1).then_inc(pool_const, 1)
            done(gp.memset(ident2[:, :, :], 0.0))
            gp.affine_select(out=ident2[:, :, :], in_=ident2[:, :, :], compare_op=ALU.not_equal, fill=1.0, base=0,
                             pattern=[[0, 2], [-1, K]], channel_multiplier=1).then_inc(pool_const, 1)
            done(gp.memset(tri[:, :], 1.0))
            gp.affine_select(out=tri[:, :], in_=tri[:, :], compare_op=ALU.is_ge, fill=0.0, base=0,
                             pattern=[[1, K]], channel_multiplier=-1).then_inc(pool_const, 1)
            gp.memset(ones[:, :], 1.0).then_inc(pool_const, 1)
            done(gp.memset(head_of[:, :], 1.0))
            done(gp.affine_select(out=head_of[:, :], in_=head_of[:, :], compare_op=ALU.is_ge, fill=0.0, base=0,
                                  pattern=[[-HD, HG]], channel_multiplier=1))
            gp.affine_select(out=head_of[:, :], in_=head_of[:, :], compare_op=ALU.is_ge, fill=0.0, base=HD - 1,
                             pattern=[[HD, HG]], channel_multiplier=-1).then_inc(pool_const, 1)
            gp.memset(minus_half[:, :], -0.5).then_inc(pool_const, 1)
            gp.memset(vals[:, :, :], 0.0).then_inc(vals_zero, 1)
            pool.wait_ge(pool_const, 6)

            def power(g, n):
                for half in range(2):
                    tiles = slice(half * 2, half * 2 + 2)
                    pool.wait_ge((ln1_var, ln2_var)[n], g * 2 + half + 1)
                    gp.tensor_tensor(rstd[:, n, tiles], var_eps[:, n, tiles], minus_half[:, tiles],
                                     ALU.pow).then_inc((rstd1_ready, rstd2_ready)[n], 1)

            def add_bo(g):
                xg = group(g)
                pool.wait_ge(xn_ready, g * B + B)
                alone(pool)
                for t in range(B):
                    last = gp.tensor_tensor(xg[:, t, :], xg[:, t, :], bo_g[:, :], ALU.add)
                last.then_inc(xb_ready, 1)

            def split(hi, lo, count):
                alone(pool)
                for n in range(4):
                    part = slice(n * 512, (n + 1) * 512)
                    gp.tensor_scalar(hi[:, part], w_raw[:, part], 1.0, 0.0, ALU.mult, ALU.add).then_inc(hi_parts, 1)
                for n in range(4):
                    part = slice(n * 512, (n + 1) * 512)
                    pool.wait_ge(hi_parts, count * 4 + n + 1)
                    last = gp.tensor_tensor(lo[:, part], w_raw[:, part], hi[:, part].bitcast(F32), ALU.subtract)
                last.then_inc(w_split, 1)

            hi_parts = sem("hi_parts")

            def split_w1(e):
                pool.wait_ge(w_loaded, e * 32 + 16)
                split(w1_hi[:, :, :].rearrange("p c f -> p (c f)"), w1_lo[:, :, :].rearrange("p c f -> p (c f)"), e * 2)

            def split_w2(e):
                pool.wait_ge(w_loaded, e * 32 + 32)
                pool.wait_ge(final_done, e * B + B)
                split(w2_hi[:, :, :].rearrange("p c f -> p (c f)"), w2_lo[:, :, :].rearrange("p c f -> p (c f)"), e * 2 + 1)

            def add_b2(g):
                pool.wait_ge(b2_loaded, g * 16 + 16)
                alone(pool)
                gp.tensor_scalar(b2_g[:, :], b2_sb[:, :], gate[:, 1:2], 0.0, ALU.mult, ALU.add).then_inc(b2g_ready, 1)
                pool.wait_ge(b2g_ready, g + 1)
                pool.wait_ge(x1n_ready, g * B + B)
                alone(pool)
                xg = group(g)
                for t in range(B):
                    last = gp.tensor_tensor(xg[:, t, :], xg[:, t, :], b2_g[:, :], ALU.add)
                last.then_inc(x1b_ready, 1)

            b2g_ready = sem("b2g_ready")

            power(0, 0)
            pool.wait_ge(bo_ready, 1)
            add_bo(0)
            split_w1(0)
            power(1, 0)
            power(0, 1)
            add_bo(1)
            add_b2(0)

            def iteration(e, g, more):
                split_w2(e)
                if more:
                    power(g + 1, 0)
                pool.wait_ge(h_ps_ready, e * FC + FC)
                split_w1(g)
                power(g, 1)
                if more:
                    add_bo(g + 1)
                add_b2(g)

            with pool.Fori(0, E - 2) as i:
                iteration(i, i + 1, True)
            iteration(E - 2, E - 1, False)
            split_w2(E - 1)

        @block.tensor
        def _(pe):
            mm = nc.tensor.matmul

            def passes(o, w_hi, w_lo, m_hi, m_lo, start, stop):
                mm(o, w_hi, m_hi, start=start, stop=False)
                mm(o, w_hi, m_lo, start=False, stop=False)
                return mm(o, w_lo, m_hi, start=False, stop=stop)

            pe.wait_ge(pool_const, 4)
            pe.wait_ge(mask_ready, 1)
            mm(attn_ps[0][0:K, 0:1], tri[:, :], mcol[0:K, :], start=True, stop=True)
            mm(attn_ps[1][:, 0:1], ones[:, :], mcol[:, :], start=True, stop=True).then_inc(count_ps_ready, 1)
            pe.wait_ge(ctx_loaded, 64)
            for c in range(C):
                for b in range(B):
                    last = mm(trans_ps[c][:, b * P:(b + 1) * P], ctx_sb[:, b, c * P:(c + 1) * P],
                              ident2[:, :, :].rearrange("p a k -> p (a k)"), start=True, stop=True)
            last.then_inc(ctx_ps_ready, 1)
            pe.wait_ge(gsel_ready, 1)
            for c in range(C):
                for b in range(B):
                    last = mm(score_ps[c][:, b * K:(b + 1) * K], ctx_sb[:, b, c * P:(c + 1) * P],
                              gsel, start=True, stop=True)
            last.then_inc(ctx_ps_ready, 1)
            pe.wait_ge(attn_w_loaded, 64)
            pe.wait_ge(ctx_sb_ready, 2)
            for m in range(C):
                for c in range(C):
                    last = mm(hid_ps[m][:, 0:B * K], w_set[:, 0, c, m * P:(m + 1) * P], ctxG[:, c, :],
                              start=(c == 0), stop=(c == C - 1))
            last.then_inc(kv_ps_ready, 1)
            for b in range(B):
                for c in range(C):
                    last = mm(trans_ps[b // 2][:, b % 2 * D:(b % 2 + 1) * D], ctxT[:, c, b, :],
                              w_set[:, 1, c, :], start=(c == 0), stop=(c == C - 1))
            last.then_inc(kv_ps_ready, 1)
            def transposes(bank, src, ready, count, signal):
                for t in range(B):
                    pe.wait_ge(ready, count + t + 1)
                    for c in range(C):
                        last = nc.tensor.transpose(bank[c][:, t * P:(t + 1) * P], src[:, t, c * P:(c + 1) * P], ident[:, :])
                        if t == B - 1:
                            last.then_inc(signal, 1)

            def x_transposed(g):
                transposes(attn_ps, norm, xn_ready, g * B, xT_ps_ready)

            def queries(g, any_before=True):
                for m in range(C):
                    if any_before:
                        pe.wait_ge(x1_ready, (g - 1) * C + m + 1)
                    for c in range(C):
                        if m == 0:
                            pe.wait_ge(xT_ready, g * C + c + 1)
                        last = passes(score_ps[m][:, :], wq_hi[:, c, m * P:(m + 1) * P], wq_lo[:, c, m * P:(m + 1) * P],
                                      xT_hi[:, c, :], xT_lo[:, c, :], c == 0, c == C - 1)
                    last.then_inc(q_ps_ready, 1)

            def scores(g, t):
                for c in range(C):
                    if t == 0:
                        pe.wait_ge(q_ready, g * C + c + 1)
                    if t > 0:
                        pe.wait_ge(shifted, g * (B * C) + (t - 1) * C + c + 1)
                    tile = slice(t * P, (t + 1) * P)
                    passes(score_ps[c][:, :], qT_hi[:, c, tile], qT_lo[:, c, tile],
                           keys_hi[:, t, c, :, :].rearrange("p h k -> p (h k)"),
                           keys_lo[:, t, c, :, :].rearrange("p h k -> p (h k)"), True, True).then_inc(s_ps_ready, 1)

            def prob_transposed(g, t):
                pe.wait_ge(p_ready, g * B + t + 1)
                for c in range(C):
                    if t > 0:
                        pe.wait_ge(pT_ready, g * (B * C) + (t - 1) * C + c + 1)
                    for j in range(PAIRS // C):
                        pair = c * (PAIRS // C) + j
                        last = nc.tensor.transpose(trans_ps[c][:, j * P:(j + 1) * P],
                                                   prob[:, t % 2, pair * P:(pair + 1) * P], ident[:, :])
                    last.then_inc(pT_ps_ready, 1)

            def weighted_values(g, t):
                pe.wait_ge(pT_ready, g * (B * C) + t * C + C)
                if t >= 2:
                    pe.wait_ge(o_ready, g * B + t - 1)
                for j in range(PAIRS):
                    last = mm(attn_ps[t % 2][:, j * PW:j * PW + PVN], probT[:, t % 2, j, :], vals[:, t, j * PW:j * PW + PVN],
                              start=True, stop=True)
                last.then_inc(pv_ready, 1)

            def o_transposed(g):
                transposes(trans_ps, attn, o_ready, g * B, oT_ps_ready)

            def out_projection(g):
                pe.wait_ge(shifted, g * (B * C) + B * C)
                for t in range(B):
                    tile = slice(t * P, (t + 1) * P)
                    for c in range(C):
                        if t == 0:
                            pe.wait_ge(oT_ready, g * C + c + 1)
                        last = passes(score_ps[t // 2][:, t % 2 * D:(t % 2 + 1) * D], oT_hi[:, c, tile], oT_lo[:, c, tile],
                                      wo_hi[:, c, :], wo_lo[:, c, :], c == 0, c == C - 1)
                    if t % 2:
                        last.then_inc(wo_ps_ready, 1)

            def f_transposed(g):
                transposes(trans_ps, norm, x1n_ready, g * B, fT_ps_ready)

            def hidden(e, f):
                if f == 0:
                    pe.wait_ge(w_split, e * 2 + 1)
                if f < 2:
                    pe.wait_ge(final_done, e * B + B - 1 + f)
                if f >= 2:
                    pe.wait_ge(gelu_done, e * FC + f - 1)
                chunk = slice(f * P, (f + 1) * P)
                for c in range(C):
                    if f == 0:
                        pe.wait_ge(fT_ready, e * C + c + 1)
                    last = passes(hid_ps[f % 2][:, :], w1_hi[:, c, chunk], w1_lo[:, c, chunk],
                                  fT_hi[:, c, :], fT_lo[:, c, :], c == 0, c == C - 1)
                last.then_inc(h_ps_ready, 1)

            def ffn_out(e, t, start, end):
                if t == 0 and start == 0:
                    pe.wait_ge(w_split, e * 2 + 2)
                if t < 2 and start == 0:
                    pe.wait_ge(gelu_done, e * FC + FC - 1 + t)
                if t >= 2 and start == 0:
                    pe.wait_ge(final_done, e * B + B + t - 1)
                tile = slice(t * P, (t + 1) * P)
                for f in range(start, end):
                    if t == 0:
                        pe.wait_ge(h_ready, e * FC + f + 1)
                    last = passes(y_ps[t % 2], hT_hi[:, f, tile], hT_lo[:, f, tile],
                                  w2_hi[:, f, :], w2_lo[:, f, :], f == 0, f == FC - 1)
                if end == FC:
                    last.then_inc(y_ps_ready, 1)

            pe.wait_ge(vals_ready, 1)
            x_transposed(0)
            pe.wait_ge(attn_w_ready, 1)
            queries(0, False)
            pe.wait_ge(keys_ready, 1)
            scores(0, 0)
            scores(0, 1)
            prob_transposed(0, 0)
            scores(0, 2)
            weighted_values(0, 0)
            prob_transposed(0, 1)
            scores(0, 3)
            weighted_values(0, 1)
            prob_transposed(0, 2)
            weighted_values(0, 2)
            prob_transposed(0, 3)
            weighted_values(0, 3)
            o_transposed(0)
            x_transposed(1)
            out_projection(0)
            queries(1)
            f_transposed(0)

            def iteration(e, g, more):
                scores(g, 0)
                hidden(e, 0)
                hidden(e, 1)
                hidden(e, 2)
                scores(g, 1)
                for f in range(3, FC):
                    hidden(e, f)
                scores(g, 2)
                ffn_out(e, 0, 0, 6)
                ffn_out(e, 1, 0, 2)
                ffn_out(e, 0, 6, FC)
                ffn_out(e, 1, 2, 4)
                prob_transposed(g, 0)
                ffn_out(e, 1, 4, 6)
                prob_transposed(g, 1)
                weighted_values(g, 0)
                scores(g, 3)
                prob_transposed(g, 2)
                weighted_values(g, 1)
                weighted_values(g, 2)
                prob_transposed(g, 3)
                ffn_out(e, 1, 6, FC)
                ffn_out(e, 2, 0, 2)
                weighted_values(g, 3)
                ffn_out(e, 2, 2, 4)
                o_transposed(g)
                ffn_out(e, 2, 4, FC)
                if more:
                    x_transposed(g + 1)
                out_projection(g)
                ffn_out(e, 3, 0, 4)
                if more:
                    queries(g + 1)
                ffn_out(e, 3, 4, FC)
                f_transposed(g)

            with pe.Fori(0, E - 2) as i:
                iteration(i, i + 1, True)
            iteration(E - 2, E - 1, False)
            for f in range(FC):
                hidden(E - 1, f)
            for t in range(B):
                ffn_out(E - 1, t, 0, FC)

        @block.scalar
        def _(act):
            activation = nc.scalar.activation
            act.wait_ge(consts_loaded, 16 * 7)
            activation(gate[:, :], gates[:, :], ACT.Tanh).then_inc(gate_ready, 1)
            act.wait_ge(ctx_ps_ready, 1)
            for c in range(C):
                last = activation(ctxT[:, c, :, :], trans_ps[c][:, :].rearrange("p (b k) -> p b k", b=B), ACT.Copy)
            last.then_inc(ctx_sb_ready, 1)
            act.wait_ge(ctx_ps_ready, 2)
            for c in range(C):
                last = activation(ctxG[:, c, :], score_ps[c][:, 0:B * K], ACT.Copy)
            last.then_inc(ctx_sb_ready, 1)
            act.wait_ge(attn_w_loaded, 64)
            for w, n in ((wq_hi, 2), (wo_hi, 3)):
                last = activation(w[:, :, :], w_set[:, n, :, :], ACT.Copy)
            last.then_inc(wq_hi_ready, 1)
            act.wait_ge(kT_ready, 1)
            for c in range(C):
                for h in range(HG):
                    last = activation(keys_hi[:, :, c, h, :], kT[:, c, :, :], ACT.Copy, scale=head_of[:, h:h + 1])
                last.then_inc(keys_hi_ready, 1)

            def x_hi(g):
                for c in range(C):
                    act.wait_ge(xT_ps_ready, g * C + c + 1)
                    activation(xT_hi[:, c, :], attn_ps[c][:, :], ACT.Copy).then_inc(xT_hi_ready, 1)

            def q_hi(g):
                for c in range(C):
                    act.wait_ge(q_ps_ready, g * C + c + 1)
                    activation(qT_hi[:, c, :], score_ps[c][:, :], ACT.Identity, bias=bq_sb[:, c:c + 1]).then_inc(q_hi_ready, 1)

            def exps(g, t):
                act.wait_ge(shifted, g * (B * C) + t * C + C)
                activation(prob[:, t % 2, :], prob[:, t % 2, :], ACT.Exp).then_inc(p_ready, 1)

            def prob_out(g, t):
                if t >= 2:
                    act.wait_ge(pv_ready, g * B + t - 1)
                for c in range(C):
                    act.wait_ge(pT_ps_ready, g * (B * C) + t * C + c + 1)
                    activation(probT[:, t % 2, c * (PAIRS // C):(c + 1) * (PAIRS // C), :],
                               trans_ps[c][:, :].rearrange("p (j q) -> p j q", q=P), ACT.Copy).then_inc(pT_ready, 1)

            def o_hi(g):
                for c in range(C):
                    act.wait_ge(oT_ps_ready, g * C + c + 1)
                    activation(oT_hi[:, c, :], trans_ps[c][:, :], ACT.Copy).then_inc(oT_hi_ready, 1)

            def f_hi(g):
                for c in range(C):
                    act.wait_ge(fT_ps_ready, g * C + c + 1)
                    activation(fT_hi[:, c, :], trans_ps[c][:, :], ACT.Copy).then_inc(fT_hi_ready, 1)

            def gelu(e, f):
                act.wait_ge(h_ps_ready, e * FC + f + 1)
                if f >= 2:
                    act.wait_ge(h_ready, e * FC + f - 1)
                activation(hid[:, f % 2, :], hid_ps[f % 2][:, :], ACT.Gelu,
                           bias=b1_bias(e, f)).then_inc(gelu_done, 1)

            def b1_bias(e, f):
                return b1_sb[:, bass.ds(e, 1), f]

            def h_hi(e, f):
                act.wait_ge(gelu_done, e * FC + f + 1)
                activation(hT_hi[:, f, :], hid[:, f % 2, :], ACT.Copy).then_inc(h_hi_ready, 1)

            x_hi(0)
            q_hi(0)
            exps(0, 0)
            exps(0, 1)
            prob_out(0, 0)
            exps(0, 2)
            prob_out(0, 1)
            exps(0, 3)
            prob_out(0, 2)
            prob_out(0, 3)
            o_hi(0)
            x_hi(1)
            q_hi(1)
            f_hi(0)

            def iteration(e, g, more):
                nc.scalar.preload_act_table(ACT.Gelu)
                for f in range(FC):
                    gelu(e, f)
                    h_hi(e, f)
                nc.scalar.preload_act_table(ACT.Exp)
                exps(g, 0)
                exps(g, 1)
                prob_out(g, 0)
                prob_out(g, 1)
                exps(g, 2)
                prob_out(g, 2)
                exps(g, 3)
                prob_out(g, 3)
                o_hi(g)
                if more:
                    x_hi(g + 1)
                    q_hi(g + 1)
                f_hi(g)

            with act.Fori(0, E - 2) as i:
                iteration(i, i + 1, True)
            iteration(E - 2, E - 1, False)
            nc.scalar.preload_act_table(ACT.Gelu)
            for f in range(FC):
                gelu(E - 1, f)
                h_hi(E - 1, f)

        @block.vector
        def _(dve):
            v = nc.vector
            self_count = [0]

            def done(ins):
                self_count[0] += 1
                ins.then_inc(dve_self, 1)
                dve.wait_ge(dve_self, self_count[0])

            dve.sem_inc(final_done, B)
            dve.wait_ge(ctx_loaded, 64)
            v.tensor_scalar(mcol[:, :], mcol_i[:, :], 0.0, None, ALU.not_equal).then_inc(mask_ready, 1)
            done(v.tensor_scalar(mrow, mrow_i[:, :], 0.0, None, ALU.not_equal))
            dve.wait_ge(pool_const, 5)
            dve.wait_ge(mask_ready, 1)
            done(v.tensor_tensor(gdiag, ident[0:K, 0:K], mrow, ALU.mult))
            dve.wait_ge(count_ps_ready, 1)
            done(v.scalar_tensor_tensor(first[:, :], attn_ps[0][0:K, 0:1], 1.0, mcol[0:K, :], ALU.is_equal, ALU.mult))
            done(v.scalar_tensor_tensor(wcol[:, :], attn_ps[1][:, 0:1], 0.0, mcol[:, :], ALU.is_equal, ALU.add))
            done(v.tensor_scalar(mrow, mrow, -1.0, 1.0, ALU.mult, ALU.add))
            v.scalar_tensor_tensor(gsel, mrow, first[:, 0:1], gdiag, ALU.mult, ALU.add).then_inc(gsel_ready, 1)
            dve.wait_ge(gate_ready, 1)
            v.tensor_scalar(bo_g[:, :], bo_sb, gate[:, 0:1], None, ALU.mult).then_inc(bo_ready, 1)
            done(v.tensor_scalar(bv_w, bv_sb, wcol[:, 0:1], None, ALU.mult))

            def stats(g, n, half):
                xg = group(g)
                done = g * 4 + half * 2
                alone(dve)
                for t in (half * 2, half * 2 + 1):
                    last = v.bn_stats(stat6[:, t, :], xg[:, t, :])
                last.then_inc(stats_done[n], 1)
                dve.wait_ge(stats_done[n], done + 1)
                alone(dve)
                for t in (half * 2, half * 2 + 1):
                    last = v.bn_aggr(stat2[:, n, t, :], stat6[:, t, :])
                last.then_inc(stats_done[n], 1)
                dve.wait_ge(stats_done[n], done + 2)
                v.tensor_scalar(var_eps[:, n, half * 2:half * 2 + 2], stat2[:, n, half * 2:half * 2 + 2, 1], EPS, None,
                                ALU.add).then_inc((ln1_var, ln2_var)[n], 1)

            def scaled(g, n):
                xg = group(g)
                for t in range(B):
                    if t % 2 == 0:
                        dve.wait_ge((rstd1_ready, rstd2_ready)[n], g * 2 + t // 2 + 1)
                    v.tensor_scalar(norm[:, t, :], xg[:, t, :], stat2[:, n, t, 0:1], rstd[:, n, t:t + 1],
                                    ALU.subtract, ALU.mult).then_inc((xn_ready, x1n_ready)[n], 1)

            stats_done = [sem("stats1_done"), sem("stats2_done")]
            dve.wait_ge(x0_loaded, 16)
            stats(0, 0, 0)
            stats(0, 0, 1)
            scaled(0, 0)
            dve.wait_ge(wq_hi_ready, 1)
            for lo, hi, n in ((wq_lo, wq_hi, 2), (wo_lo, wo_hi, 3)):
                last = v.tensor_tensor(lo[:, :, :], w_set[:, n, :, :], hi[:, :, :].bitcast(F32), ALU.subtract)
            last.then_inc(attn_w_ready, 1)
            dve.wait_ge(kv_ps_ready, 1)
            for c in range(C):
                last = v.tensor_scalar(kT[:, c, :, :], hid_ps[c][:, 0:B * K].rearrange("p (b k) -> p b k", b=B),
                                       bk_sb[:, c:c + 1], SCALE, ALU.add, ALU.mult)
            last.then_inc(kT_ready, 1)
            dve.wait_ge(kT_ready, 1)
            dve.wait_ge(kv_ps_ready, 2)
            dve.wait_ge(vals_zero, 1)
            for b in range(B):
                for side in range(2):
                    rows = slice(side * K, (side + 1) * K)
                    dst = vals[rows, b, 0:PAIRS * PW].rearrange("p (j n) -> p j n", n=PW)
                    src = trans_ps[b // 2][rows, b % 2 * D:(b % 2 + 1) * D].rearrange("p (j n) -> p j n", n=2 * HD)
                    bias = bv_w[rows, :].rearrange("p (j n) -> p j n", n=2 * HD)
                    cols = slice(side * HD, (side + 1) * HD)
                    v.scalar_tensor_tensor(dst[:, :, cols], src[:, :, cols], wcol[rows, 0:1], bias[:, :, cols],
                                           ALU.mult, ALU.add)
                    last = v.tensor_scalar(dst[:, :, 2 * HD + side:2 * HD + side + 1],
                                           ones[rows, 0:PAIRS].unsqueeze(2), wcol[rows, 0:1], None, ALU.mult)
            last.then_inc(vals_ready, 1)
            for c in range(C):
                dve.wait_ge(keys_hi_ready, c + 1)
                for h in range(HG):
                    last = v.scalar_tensor_tensor(keys_lo[:, :, c, h, :], kT[:, c, :, :], head_of[:, h:h + 1],
                                                  keys_hi[:, :, c, h, :].bitcast(F32), ALU.mult, ALU.subtract)
            last.then_inc(keys_ready, 1)

            def lo_part(lo, hi, ps, hi_ready, signal, g):
                for c in range(C):
                    dve.wait_ge(hi_ready, g * C + c + 1)
                    v.tensor_tensor(lo[:, c, :], ps[c][:, :], hi[:, c, :].bitcast(F32), ALU.subtract).then_inc(signal, 1)

            def q_lo(g):
                for c in range(C):
                    dve.wait_ge(q_hi_ready, g * C + c + 1)
                    v.scalar_tensor_tensor(qT_lo[:, c, :], score_ps[c][:, :], bq_sb[:, c:c + 1],
                                           qT_hi[:, c, :].bitcast(F32), ALU.add, ALU.subtract).then_inc(q_ready, 1)

            max_done = sem("max_done")
            rden_done = sem("rden_done")

            def shift(g, t):
                if t >= 2:
                    dve.wait_ge(pT_ps_ready, g * (B * C) + (t - 1) * C)
                for c in range(C):
                    dve.wait_ge(s_ps_ready, g * (B * C) + t * C + c + 1)
                    v.tensor_reduce(smax[:, t % 2, c * HG:(c + 1) * HG],
                                    score_ps[c][:, :].rearrange("p (h k) -> p h k", k=K), AX_X, ALU.max).then_inc(max_done, 1)
                for c in range(C):
                    dve.wait_ge(max_done, g * (B * C) + t * C + c + 1)
                    v.tensor_tensor(prob[:, t % 2, c * TOK:(c + 1) * TOK].rearrange("p (h k) -> p h k", k=K),
                                    score_ps[c][:, :].rearrange("p (h k) -> p h k", k=K),
                                    smax[:, t % 2, c * HG:(c + 1) * HG].unsqueeze(2).to_broadcast([P, HG, K]),
                                    ALU.subtract).then_inc(shifted, 1)

            def normalise(g, t):
                if t >= 2:
                    dve.wait_ge(o_ready, g * B + t - 1)
                dve.wait_ge(pv_ready, g * B + t + 1)
                pairs = attn_ps[t % 2][:, 0:PAIRS * PW].rearrange("p (j n) -> p j n", n=PW)
                v.reciprocal(rden[:, t % 2, :].rearrange("p (j a) -> p j a", a=2), pairs[:, :, 2 * HD:PW]).then_inc(rden_done, 1)
                dve.wait_ge(rden_done, g * B + t + 1)
                v.tensor_tensor(attn[:, t, :].rearrange("p (j a d) -> p j a d", a=2, d=HD),
                                pairs[:, :, 0:2 * HD].rearrange("p j (a d) -> p j a d", a=2),
                                rden[:, t % 2, :].rearrange("p (j a) -> p j a", a=2).unsqueeze(3).to_broadcast([P, PAIRS, 2, HD]),
                                ALU.mult).then_inc(o_ready, 1)

            def residual(g):
                dve.wait_ge(xb_ready, g + 1)
                xg = group(g).rearrange("p (h b) d -> p h (b d)", h=2)
                for n in range(2):
                    dve.wait_ge(wo_ps_ready, g * 2 + n + 1)
                    v.scalar_tensor_tensor(xg[:, n, :], score_ps[n][:, :], gate[:, 0:1], xg[:, n, :],
                                           ALU.mult, ALU.add).then_inc(x1_ready, 1)
                    dve.wait_ge(x1_ready, g * 2 + n + 1)
                    stats(g, 1, n)

            def h_lo(e, f):
                dve.wait_ge(h_hi_ready, e * FC + f + 1)
                v.tensor_tensor(hT_lo[:, f, :], hid[:, f % 2, :], hT_hi[:, f, :].bitcast(F32), ALU.subtract).then_inc(h_ready, 1)

            def final(e, t):
                if t == 0:
                    dve.wait_ge(x1b_ready, e + 1)
                dve.wait_ge(y_ps_ready, e * B + t + 1)
                xg = group(e)
                v.scalar_tensor_tensor(xg[:, t, :], y_ps[t % 2], gate[:, 1:2], xg[:, t, :],
                                       ALU.mult, ALU.add).then_inc(final_done, 1)

            def x_scaled(g):
                scaled(g, 0)

            def x_lo(g):
                lo_part(xT_lo, xT_hi, attn_ps, xT_hi_ready, xT_ready, g)

            def o_lo(g):
                lo_part(oT_lo, oT_hi, trans_ps, oT_hi_ready, oT_ready, g)

            def f_lo(g):
                lo_part(fT_lo, fT_hi, trans_ps, fT_hi_ready, fT_ready, g)

            x_lo(0)
            q_lo(0)
            shift(0, 0)
            shift(0, 1)
            dve.wait_ge(x_loaded, 16)
            stats(1, 0, 0)
            stats(1, 0, 1)
            x_scaled(1)
            shift(0, 2)
            normalise(0, 0)
            shift(0, 3)
            normalise(0, 1)
            normalise(0, 2)
            normalise(0, 3)
            o_lo(0)
            x_lo(1)
            residual(0)
            scaled(0, 1)
            q_lo(1)
            f_lo(0)

            def iteration(e, g, more):
                shift(g, 0)
                h_lo(e, 0)
                h_lo(e, 1)
                shift(g, 1)
                for f in range(2, FC):
                    h_lo(e, f)
                final(e, 0)
                shift(g, 2)
                normalise(g, 0)
                if more:
                    stats(g + 1, 0, 0)
                shift(g, 3)
                if more:
                    stats(g + 1, 0, 1)
                normalise(g, 1)
                normalise(g, 2)
                if more:
                    x_scaled(g + 1)
                final(e, 1)
                normalise(g, 3)
                o_lo(g)
                final(e, 2)
                if more:
                    x_lo(g + 1)
                residual(g)
                scaled(g, 1)
                if more:
                    q_lo(g + 1)
                final(e, 3)
                f_lo(g)

            with dve.Fori(0, E - 2) as i:
                iteration(i, i + 1, True)
            iteration(E - 2, E - 1, False)
            for f in range(FC):
                h_lo(E - 1, f)
            for t in range(B):
                final(E - 1, t)


def kernel(x, ctx_1024, mask_1xS2_if1, g_xattn, g_ffn, L0_xattn_Wq, L0_xattn_bq, L0_xattn_Wk, L0_xattn_bk,
           L0_xattn_Wv, L0_xattn_bv, L0_xattn_Wo, L0_xattn_bo, L0_ffn_w1, L0_ffn_b1, L0_ffn_w2, L0_ffn_b2):
    import numpy as np
    import concourse.bacc as bacc
    from concourse.bass_utils import run_bass_kernel_spmd

    def halves(w):
        return np.ascontiguousarray(np.asarray(w).reshape(C, P, -1).transpose(1, 0, 2))

    def column(b):
        return np.ascontiguousarray(np.asarray(b).reshape(C, P).T)

    def row(b):
        return np.ascontiguousarray(np.asarray(b).reshape(1, -1))

    arrays = {
        "x": np.ascontiguousarray(np.asarray(x).reshape(B, E, P, D).transpose(1, 2, 0, 3)).reshape(E, P, B * D),
        "ctx": np.ascontiguousarray(np.asarray(ctx_1024).transpose(1, 0, 2)),
        "mask": np.ascontiguousarray(np.asarray(mask_1xS2_if1)),
        "g_x": row(g_xattn), "g_f": row(g_ffn),
        "wq": halves(L0_xattn_Wq), "bq": column(L0_xattn_bq),
        "wk": halves(L0_xattn_Wk), "bk": column(L0_xattn_bk),
        "wv": halves(L0_xattn_Wv), "bv": row(L0_xattn_bv),
        "wo": halves(L0_xattn_Wo), "bo": row(L0_xattn_bo),
        "w1": np.ascontiguousarray(np.asarray(L0_ffn_w1).reshape(E, F, C, P).transpose(0, 3, 2, 1)).reshape(E, P, C * F),
        "b1": np.ascontiguousarray(np.asarray(L0_ffn_b1).reshape(E, FC, P).transpose(2, 0, 1)),
        "w2": np.ascontiguousarray(np.asarray(L0_ffn_w2).reshape(E, D, FC, P).transpose(0, 3, 2, 1)).reshape(E, P, FC * D),
        "b2": np.ascontiguousarray(np.asarray(L0_ffn_b2)),
    }
    nc = bacc.Bacc("TRN2", target_bir_lowering=False, num_devices=1)
    feeds = {f"in_{n}": a for n, a in arrays.items()}
    args = [nc.dram_tensor(n, a.shape, mybir.dt.from_np(a.dtype), kind="ExternalInput").ap() for n, a in feeds.items()]
    out = nc.dram_tensor("out", (E, P, B * D), F32, kind="ExternalOutput").ap()
    build(nc, *args, out)
    r = run_bass_kernel_spmd(nc, [feeds], core_ids=[0])
    got = r.results[0]["out"].reshape(E, P, B, D).transpose(2, 0, 1, 3).reshape(B, S, D)
    return np.ascontiguousarray(got)
```

```python
from contextlib import ExitStack

import concourse.bass as bass
from concourse import mybir

F32 = mybir.dt.float32
F32R = mybir.dt.float32r
I32 = mybir.dt.int32
ALU = mybir.AluOpType
ACT = mybir.ActivationFunctionType
AX_X = mybir.AxisListType.X

P = 128
D = 256
C = D // P
B = 4
S = 1024
E = S // P
TOK = B * P
F = 1024
FC = F // P
H = 16
HD = D // H
K = 64
HG = H // C
PAIRS = H // 2
PW = 2 * HD + 2
PVN = 96
EPS = 1e-5
POOL_HI_HEAD, POOL_LO_HEAD = 4, 6
SCALE = 0.25


def build(nc, x, ctx, mask, g_x, g_f, wq, bq, wk, bk, wv, bv, wo, bo, w1, b1, w2, b2, out):
    stack = ExitStack()
    with stack:
        def sb(name, shape, dt=F32):
            return stack.enter_context(nc.sbuf_tensor(name, shape, dt))

        def sem(name):
            return stack.enter_context(nc.semaphore(name))

        xs = sb("xs", [P, E * B * D])
        attn = sb("attn", [P, B, D])
        norm = sb("norm", [P, B, D])
        xT_hi = sb("xT_hi", [P, C, TOK], F32R)
        xT_lo = sb("xT_lo", [P, C, TOK], F32R)
        fT_hi = sb("fT_hi", [P, C, TOK], F32R)
        fT_lo = sb("fT_lo", [P, C, TOK], F32R)
        qT_hi = sb("qT_hi", [P, C, TOK], F32R)
        qT_lo = sb("qT_lo", [P, C, TOK], F32R)
        oT_hi, oT_lo = qT_hi, qT_lo
        prob = sb("prob", [P, 2, H * K])
        probT = sb("probT", [P, 2, PAIRS, P])
        hid = sb("hid", [P, 2, TOK])
        hT_hi = sb("hT_hi", [P, FC, TOK], F32R)
        hT_lo = sb("hT_lo", [P, FC, TOK], F32R)
        w_raw = sb("w_raw", [P, C * F])
        w1_hi = sb("w1_hi", [P, C, F], F32R)
        w1_lo = sb("w1_lo", [P, C, F], F32R)
        w2_hi = sb("w2_hi", [P, FC, D], F32R)
        w2_lo = sb("w2_lo", [P, FC, D], F32R)
        wq_hi = sb("wq_hi", [P, C, D], F32R)
        wq_lo = sb("wq_lo", [P, C, D], F32R)
        wo_hi = sb("wo_hi", [P, C, D], F32R)
        wo_lo = sb("wo_lo", [P, C, D], F32R)
        keys_hi = sb("keys_hi", [P, B, C, HG, K], F32R)
        keys_lo = sb("keys_lo", [P, B, C, HG, K], F32R)
        vals = sb("vals", [P, B, (PAIRS - 1) * PW + PVN])
        ident = sb("ident", [P, P])
        b1_sb = sb("b1_sb", [P, E, FC])
        b2_sb = sb("b2_sb", [P, D])
        b2_g = sb("b2_g", [P, D])
        bo_g = sb("bo_g", [P, D])
        bq_sb = sb("bq_sb", [P, C])
        bk_sb = sb("bk_sb", [P, C])
        gates = sb("gates", [P, 2])
        gate = sb("gate", [P, 2])
        head_of = sb("head_of", [P, HG])
        minus_half = sb("minus_half", [P, B])
        stat6 = sb("stat6", [P, B, 6])
        stat2 = sb("stat2", [P, 2, B, 2])
        var_eps = sb("var_eps", [P, 2, B])
        rstd = sb("rstd", [P, 2, B])
        smax = sb("smax", [P, 2, H])
        rden = sb("rden", [P, 2, H])
        mcol_i = sb("mcol_i", [P, 1], I32)
        mcol = sb("mcol", [P, 1])
        wcol = sb("wcol", [P, 1])
        first = sb("first", [K, 1])
        w_set = prob[:, :, :].rearrange("p a (n c d) -> p (a n) c d", n=2, c=C)
        kT_hi = hT_hi[:, 0, :].rearrange("p (c b k) -> p c b k", c=C, b=B)
        kT_lo = hT_hi[:, 1, :].rearrange("p (c b k) -> p c b k", c=C, b=B)
        ctx_sb = probT[0:K, 0, :, :].rearrange("p j q -> p (j q)").rearrange("p (b d) -> p b d", b=B)
        ctxT = probT[:, 1, :, :].rearrange("p j q -> p (j q)").rearrange("p (c b k) -> p c b k", c=C, b=B)
        ctxG = hid[:, 0, :].rearrange("p (c n) -> p c n", c=C)
        kT = hid[:, 1, :].rearrange("p (c b k) -> p c b k", c=C, b=B)
        bv_sb = attn[:, 0, :]
        bv_w = attn[:, 1, :]
        bo_sb = attn[:, 2, :]
        small = attn[0:K, 3, :]
        mrow = small[:, 0:K]
        gsel = small[:, K:2 * K]
        gdiag = small[:, 2 * K:3 * K]
        mrow_i = sb("mrow_i", [K, K], I32)
        tri = sb("tri", [K, K])
        ones = sb("ones", [P, P])
        ident2 = sb("ident2", [K, 2, K])

        score_ps = [stack.enter_context(nc.psum_tensor(f"score_ps{i}", [P, TOK], F32)) for i in range(2)]
        trans_ps = [stack.enter_context(nc.psum_tensor(f"trans_ps{i}", [P, TOK], F32)) for i in range(2)]
        hid_ps = [stack.enter_context(nc.psum_tensor(f"hid_ps{i}", [P, TOK], F32)) for i in range(2)]
        attn_ps = [stack.enter_context(nc.psum_tensor(f"attn_ps{i}", [P, TOK], F32)) for i in range(2)]
        y_ps = [bank[:, 0:D] for bank in hid_ps] * 2
        y_last_ps = [bank[:, 0:D] for bank in score_ps + hid_ps]

        x0_loaded, x1_loaded, x_loaded, w_loaded, b2_loaded = sem("x0_loaded"), sem("x1_loaded"), sem("x_loaded"), sem("w_loaded"), sem("b2_loaded")
        mask_loaded, ctx_loaded, consts_loaded = sem("mask_loaded"), sem("ctx_loaded"), sem("consts_loaded")
        wk_loaded, wq_loaded, wv_loaded, wo_loaded = sem("wk_loaded"), sem("wq_loaded"), sem("wv_loaded"), sem("wo_loaded")
        stored = sem("stored")
        waited = sem("waited")
        pool_const, pool_self, dve_self, act_self = sem("pool_const"), sem("pool_self"), sem("dve_self"), sem("act_self")
        mask_ready, count_ps_ready, gsel_ready = sem("mask_ready"), sem("count_ps_ready"), sem("gsel_ready")
        ctx_ps_ready, ctx_sb_ready, kv_ps_ready = sem("ctx_ps_ready"), sem("ctx_sb_ready"), sem("kv_ps_ready")
        kT_ready, kT_hi_ready, kT_lo_ready = sem("kT_ready"), sem("kT_hi_ready"), sem("kT_lo_ready")
        keys_hi_ready, keys_lo_ready = sem("keys_hi_ready"), sem("keys_lo_ready")
        vals_zero, wcol_ready, vals_ones_ready, vals_scaled, bv_ready, vals_ready = sem("vals_zero"), sem("wcol_ready"), sem("vals_ones_ready"), sem("vals_scaled"), sem("bv_ready"), sem("vals_ready")
        gate_ready, bo_ready, wq_ready, wo_ready = sem("gate_ready"), sem("bo_ready"), sem("wq_ready"), sem("wo_ready")
        ln1_var, rstd1_ready, xn_ready, xb_ready = sem("ln1_var"), sem("rstd1_ready"), sem("xn_ready"), sem("xb_ready")
        xT_ps_ready, xT_hi_ready, xT_ready = sem("xT_ps_ready"), sem("xT_hi_ready"), sem("xT_ready")
        q_ps_ready, q_hi_ready, q_ready = sem("q_ps_ready"), sem("q_hi_ready"), sem("q_ready")
        s_ps_ready, shifted, p_ready = sem("s_ps_ready"), sem("shifted"), sem("p_ready")
        pT_ps_ready, pT_ready, pv_ready, o_ready = sem("pT_ps_ready"), sem("pT_ready"), sem("pv_ready"), sem("o_ready")
        oT_ps_ready, oT_hi_ready, oT_ready = sem("oT_ps_ready"), sem("oT_hi_ready"), sem("oT_ready")
        wo_ps_ready, x1_ready, ln2_var, rstd2_ready, x1n_ready, x1b_ready = sem("wo_ps_ready"), sem("x1_ready"), sem("ln2_var"), sem("rstd2_ready"), sem("x1n_ready"), sem("x1b_ready")
        fT_ps_ready, fT_hi_ready, fT_ready = sem("fT_ps_ready"), sem("fT_hi_ready"), sem("fT_ready")
        h_ps_ready, gelu_done, h_hi_ready, h_ready = sem("h_ps_ready"), sem("gelu_done"), sem("h_hi_ready"), sem("h_ready")
        y_ps_ready, final_done, w_split = sem("y_ps_ready"), sem("final_done"), sem("w_split")

        def group(g, n=1):
            return xs[:, bass.ds(g * (B * D), B * D)].rearrange("p (b d) -> p b d", b=B)

        def alone(engine):
            engine.sem_inc(waited, 1)

        block = stack.enter_context(nc.Block())

        @block.sync
        def _(sp):
            def load_w(src, e):
                sp.dma_start(w_raw[:, :], src[bass.ds(e, 1), :, :].rearrange("e p n -> p (e n)")).then_inc(w_loaded, 16)

            def load_b2(e):
                sp.dma_start(b2_sb[:, :], b2[bass.ds(e, 1), :].to_broadcast([P, D])).then_inc(b2_loaded, 16)

            def store(e):
                sp.dma_start(out[bass.ds(e, 1), :, :].rearrange("e p n -> p (e n)"),
                             xs[:, bass.ds(e * (B * D), B * D)]).then_inc(stored, 16)

            sp.dma_start(mrow_i[:, :], mask.to_broadcast([K, K])).then_inc(mask_loaded, 16)
            for half in range(2):
                sp.dma_start(mcol_i[half * K:(half + 1) * K, :], mask.rearrange("o k -> k o")).then_inc(mask_loaded, 16)
            sp.dma_start(ctx_sb, ctx).then_inc(ctx_loaded, 16)
            sp.dma_start(xs[:, 0:B * D], x[0, :, :]).then_inc(x0_loaded, 16)
            sp.dma_start(w_set[:, 0, :, :], wk).then_inc(wk_loaded, 16)
            sp.dma_start(bk_sb[:, :], bk).then_inc(wk_loaded, 16)
            sp.dma_start(w_set[:, 1, :, :], wq).then_inc(wq_loaded, 16)
            sp.dma_start(bq_sb[:, :], bq).then_inc(wq_loaded, 16)
            sp.dma_start(w_set[:, 2, :, :], wv).then_inc(wv_loaded, 16)
            sp.dma_start(bv_sb, bv.to_broadcast([P, D])).then_inc(wv_loaded, 16)
            sp.dma_start(xs[:, B * D:2 * B * D], x[1, :, :]).then_inc(x1_loaded, 16)
            sp.dma_start(w_set[:, 3, :, :], wo).then_inc(wo_loaded, 16)
            sp.dma_start(bo_sb, bo.to_broadcast([P, D])).then_inc(consts_loaded, 16)
            sp.dma_start(gates[:, 0:1], g_x.to_broadcast([P, 1])).then_inc(consts_loaded, 16)
            sp.dma_start(gates[:, 1:2], g_f.to_broadcast([P, 1])).then_inc(consts_loaded, 16)
            sp.dma_start(b1_sb[:, :, :], b1).then_inc(consts_loaded, 16)
            load_w(w1, 0)
            load_b2(0)
            sp.dma_start(xs[:, 2 * B * D:E * B * D].rearrange("p (e n) -> p e n", e=E - 2),
                         x[2:E, :, :].rearrange("e p n -> p e n")).then_inc(x_loaded, 16)
            sp.wait_ge(w_split, 1)
            load_w(w2, 0)
            with sp.Fori(0, E - 1) as i:
                sp.wait_ge(w_split, i * 2 + 2)
                load_w(w1, i + 1)
                sp.wait_ge(x1b_ready, i + 1)
                load_b2(i + 1)
                sp.wait_ge(w_split, i * 2 + 3)
                load_w(w2, i + 1)
                sp.wait_ge(final_done, i * B + 2 * B)
                store(i)
            last = xs[:, (E - 1) * B * D:E * B * D]
            sp.wait_ge(final_done, E * B + B - 1)
            sp.dma_start(out[E - 1, :, 0:(B - 1) * D], last[:, 0:(B - 1) * D]).then_inc(stored, 16)
            sp.wait_ge(final_done, E * B + B)
            sp.dma_start(out[E - 1, :, (B - 1) * D:B * D], last[:, (B - 1) * D:B * D]).then_inc(stored, 16)
            sp.wait_ge(stored, (E + 1) * 16)

        @block.gpsimd
        def _(pool):
            self_count = [0]

            def done(ins):
                self_count[0] += 1
                ins.then_inc(pool_self, 1)
                pool.wait_ge(pool_self, self_count[0])

            gp = nc.gpsimd
            done(gp.memset(ident[:, :], 0.0))
            gp.affine_select(out=ident[:, :], in_=ident[:, :], compare_op=ALU.not_equal, fill=1.0, base=0,
                             pattern=[[-1, P]], channel_multiplier=1).then_inc(pool_const, 1)
            done(gp.memset(ident2[:, :, :], 0.0))
            gp.affine_select(out=ident2[:, :, :], in_=ident2[:, :, :], compare_op=ALU.not_equal, fill=1.0, base=0,
                             pattern=[[0, 2], [-1, K]], channel_multiplier=1).then_inc(pool_const, 1)
            done(gp.memset(tri[:, :], 1.0))
            gp.affine_select(out=tri[:, :], in_=tri[:, :], compare_op=ALU.is_ge, fill=0.0, base=0,
                             pattern=[[1, K]], channel_multiplier=-1).then_inc(pool_const, 1)
            gp.memset(ones[:, :], 1.0).then_inc(pool_const, 1)
            done(gp.memset(head_of[:, :], 1.0))
            done(gp.affine_select(out=head_of[:, :], in_=head_of[:, :], compare_op=ALU.is_ge, fill=0.0, base=0,
                                  pattern=[[-HD, HG]], channel_multiplier=1))
            gp.affine_select(out=head_of[:, :], in_=head_of[:, :], compare_op=ALU.is_ge, fill=0.0, base=HD - 1,
                             pattern=[[HD, HG]], channel_multiplier=-1).then_inc(pool_const, 1)
            gp.memset(minus_half[:, :], -0.5).then_inc(pool_const, 1)
            gp.memset(vals[:, :, :], 0.0).then_inc(vals_zero, 1)
            gp.memset(bv_w, 0.0).then_inc(vals_zero, 1)
            pool.wait_ge(pool_const, 6)

            def power(g, n):
                for half in range(2):
                    tiles = slice(half * 2, half * 2 + 2)
                    pool.wait_ge((ln1_var, ln2_var)[n], g * 2 + half + 1)
                    gp.tensor_tensor(rstd[:, n, tiles], var_eps[:, n, tiles], minus_half[:, tiles],
                                     ALU.pow).then_inc((rstd1_ready, rstd2_ready)[n], 1)

            def add_bo(g):
                xg = group(g)
                pool.wait_ge(xn_ready, g * B + B)
                alone(pool)
                for t in range(B):
                    last = gp.tensor_tensor(xg[:, t, :], xg[:, t, :], bo_g[:, :], ALU.add)
                last.then_inc(xb_ready, 1)

            def split(hi, lo, count):
                alone(pool)
                for n in range(4):
                    part = slice(n * 512, (n + 1) * 512)
                    gp.tensor_scalar(hi[:, part], w_raw[:, part], 1.0, 0.0, ALU.mult, ALU.add).then_inc(hi_parts, 1)
                for n in range(4):
                    part = slice(n * 512, (n + 1) * 512)
                    pool.wait_ge(hi_parts, count * 4 + n + 1)
                    last = gp.tensor_tensor(lo[:, part], w_raw[:, part], hi[:, part].bitcast(F32), ALU.subtract)
                last.then_inc(w_split, 1)

            hi_parts = sem("hi_parts")

            def split_w1(e):
                pool.wait_ge(w_loaded, e * 32 + 16)
                split(w1_hi[:, :, :].rearrange("p c f -> p (c f)"), w1_lo[:, :, :].rearrange("p c f -> p (c f)"), e * 2)

            def split_w2(e):
                pool.wait_ge(w_loaded, e * 32 + 32)
                pool.wait_ge(final_done, e * B + B)
                split(w2_hi[:, :, :].rearrange("p c f -> p (c f)"), w2_lo[:, :, :].rearrange("p c f -> p (c f)"), e * 2 + 1)

            def add_b2(g):
                pool.wait_ge(b2_loaded, g * 16 + 16)
                alone(pool)
                gp.tensor_scalar(b2_g[:, :], b2_sb[:, :], gate[:, 1:2], 0.0, ALU.mult, ALU.add).then_inc(b2g_ready, 1)
                pool.wait_ge(b2g_ready, g + 1)
                pool.wait_ge(x1n_ready, g * B + B)
                alone(pool)
                xg = group(g)
                for t in range(B):
                    last = gp.tensor_tensor(xg[:, t, :], xg[:, t, :], b2_g[:, :], ALU.add)
                last.then_inc(x1b_ready, 1)

            b2g_ready = sem("b2g_ready")

            def split_set(hi, lo, n, loaded, parts, signal):
                pool.wait_ge(*loaded)
                whole = w_set[:, n, :, :]
                gp.tensor_scalar(hi[:, :, :], whole, 1.0, 0.0, ALU.mult, ALU.add).then_inc(parts, 1)
                pool.wait_ge(parts, 1)
                gp.tensor_tensor(lo[:, :, :], whole, hi[:, :, :].bitcast(F32), ALU.subtract).then_inc(signal, 1)

            def values_bias(half):
                pool.wait_ge(vals_scaled, half + 1)
                alone(pool)
                bias = bv_w.rearrange("p (j n) -> p j n", n=2 * HD)
                for b in (half * 2, half * 2 + 1):
                    dst = vals[:, b, 0:PAIRS * PW].rearrange("p (j n) -> p j n", n=PW)[:, :, 0:2 * HD]
                    last = gp.tensor_tensor(dst, dst, bias, ALU.add)
                last.then_inc(vals_ready, 1)

            power(0, 0)
            split_set(wq_hi, wq_lo, 1, (wq_loaded, 32), sem("wq_hi_ready"), wq_ready)
            pool.wait_ge(kT_ready, 1)
            alone(pool)
            for h in range(POOL_HI_HEAD, HG):
                last = gp.tensor_scalar(keys_hi[:, :, :, h, :], kT.rearrange("p c b k -> p b c k"), head_of[:, h:h + 1], 0.0,
                                        ALU.mult, ALU.add)
            last.then_inc(keys_hi_ready, 1)
            pool.wait_ge(kT_lo_ready, 1)
            alone(pool)
            for h in range(POOL_LO_HEAD, HG):
                last = gp.tensor_scalar(keys_lo[:, :, :, h, :], kT_lo.bitcast(F32).rearrange("p c b k -> p b c k"),
                                        head_of[:, h:h + 1], 0.0, ALU.mult, ALU.add)
            last.then_inc(keys_lo_ready, 1)
            split_set(wo_hi, wo_lo, 3, (wo_loaded, 16), sem("wo_hi_ready"), wo_ready)
            pool.wait_ge(bv_ready, 1)
            values_bias(0)
            power(1, 0)
            values_bias(1)
            split_w1(0)
            pool.wait_ge(bo_ready, 1)
            add_bo(0)
            power(0, 1)
            add_bo(1)
            add_b2(0)

            def iteration(e, g, more):
                split_w2(e)
                if more:
                    power(g + 1, 0)
                pool.wait_ge(h_ps_ready, e * FC + FC)
                split_w1(g)
                power(g, 1)
                if more:
                    add_bo(g + 1)
                add_b2(g)

            with pool.Fori(0, E - 2) as i:
                iteration(i, i + 1, True)
            iteration(E - 2, E - 1, False)
            split_w2(E - 1)

        @block.tensor
        def _(pe):
            mm = nc.tensor.matmul

            def passes(o, w_hi, w_lo, m_hi, m_lo, start, stop, m_lo_ready=None, w_lo_ready=None):
                mm(o, w_hi, m_hi, start=start, stop=False)
                if m_lo_ready:
                    mm(o, w_lo, m_hi, start=False, stop=False)
                    pe.wait_ge(*m_lo_ready)
                    return mm(o, w_hi, m_lo, start=False, stop=stop)
                mm(o, w_hi, m_lo, start=False, stop=False)
                if w_lo_ready:
                    pe.wait_ge(*w_lo_ready)
                return mm(o, w_lo, m_hi, start=False, stop=stop)

            pe.wait_ge(pool_const, 4)
            pe.wait_ge(mask_ready, 1)
            mm(attn_ps[0][0:K, 0:1], tri[:, :], mcol[0:K, :], start=True, stop=True)
            mm(attn_ps[1][:, 0:1], ones[:, :], mcol[:, :], start=True, stop=True).then_inc(count_ps_ready, 1)
            pe.wait_ge(ctx_loaded, 16)
            pe.wait_ge(gsel_ready, 1)
            for c in range(C):
                for b in range(B):
                    last = mm(score_ps[c][:, b * K:(b + 1) * K], ctx_sb[:, b, c * P:(c + 1) * P],
                              gsel, start=True, stop=True)
                last.then_inc(ctx_ps_ready, 1)

            def context_transposed():
                for c in range(C):
                    for b in range(B):
                        last = mm(trans_ps[c][:, b * P:(b + 1) * P], ctx_sb[:, b, c * P:(c + 1) * P],
                                  ident2[:, :, :].rearrange("p a k -> p (a k)"), start=True, stop=True)
                last.then_inc(ctx_ps_ready, 1)

            def keys_product():
                pe.wait_ge(wk_loaded, 32)
                for m in range(C):
                    for c in range(C):
                        if m == 0:
                            pe.wait_ge(ctx_sb_ready, c + 1)
                        last = mm(hid_ps[m][:, 0:B * K], w_set[:, 0, c, m * P:(m + 1) * P], ctxG[:, c, :],
                                  start=(c == 0), stop=(c == C - 1))
                    last.then_inc(kv_ps_ready, 1)

            def values_product(half):
                pe.wait_ge(wv_loaded, 32)
                pe.wait_ge(ctx_sb_ready, C + 1)
                for b in range(2):
                    bank = attn_ps[half][:, b * D:(b + 1) * D]
                    for c in range(C):
                        last = mm(bank, ctxT[:, c, half * 2 + b, :], w_set[:, 2, c, :], start=(c == 0), stop=(c == C - 1))
                last.then_inc(kv_ps_ready, 1)

            def transposes(bank, src, ready, count, signal):
                for t in range(B):
                    pe.wait_ge(ready, count + t + 1)
                    for c in range(C):
                        last = nc.tensor.transpose(bank[c][:, t * P:(t + 1) * P], src[:, t, c * P:(c + 1) * P], ident[:, :])
                        if t == B - 1:
                            last.then_inc(signal, 1)

            def x_transposed(g, bank=attn_ps):
                transposes(bank, norm, xn_ready, g * B, xT_ps_ready)

            def queries(g, bank=score_ps, after_residual=True, chunks=range(C)):
                for m in chunks:
                    if after_residual:
                        pe.wait_ge(x1_ready, (g - 1) * C + m + 1)
                    for c in range(C):
                        if m == 0:
                            pe.wait_ge(xT_hi_ready, g * C + c + 1)
                        last = passes(bank[m][:, :], wq_hi[:, c, m * P:(m + 1) * P], wq_lo[:, c, m * P:(m + 1) * P],
                                      xT_hi[:, c, :], xT_lo[:, c, :], c == 0, c == C - 1,
                                      m_lo_ready=(xT_ready, g * C + c + 1) if m == 0 else None)
                    last.then_inc(q_ps_ready, 1)

            def scores(g, t, bank=score_ps, before=1):
                for c in range(C):
                    if t == 0:
                        pe.wait_ge(q_ready, g * C + c + 1)
                    if t >= before:
                        pe.wait_ge(shifted, g * (B * C) + (t - before) * C + c + 1)
                    tile = slice(t * P, (t + 1) * P)
                    passes(bank[c][:, :], qT_hi[:, c, tile], qT_lo[:, c, tile],
                           keys_hi[:, t, c, :, :].rearrange("p h k -> p (h k)"),
                           keys_lo[:, t, c, :, :].rearrange("p h k -> p (h k)"), True, True).then_inc(s_ps_ready, 1)

            def prob_transposed(g, t):
                pe.wait_ge(p_ready, g * B + t + 1)
                for c in range(C):
                    if t > 0:
                        pe.wait_ge(pT_ready, g * (B * C) + (t - 1) * C + c + 1)
                    for j in range(PAIRS // C):
                        pair = c * (PAIRS // C) + j
                        last = nc.tensor.transpose(trans_ps[c][:, j * P:(j + 1) * P],
                                                   prob[:, t % 2, pair * P:(pair + 1) * P], ident[:, :])
                    last.then_inc(pT_ps_ready, 1)

            def weighted_values(g, t):
                pe.wait_ge(pT_ready, g * (B * C) + t * C + C)
                if t >= 2:
                    pe.wait_ge(o_ready, g * B + t - 1)
                for j in range(PAIRS):
                    last = mm(attn_ps[t % 2][:, j * PW:j * PW + PVN], probT[:, t % 2, j, :], vals[:, t, j * PW:j * PW + PVN],
                              start=True, stop=True)
                last.then_inc(pv_ready, 1)

            def o_transposed(g):
                transposes(trans_ps, attn, o_ready, g * B, oT_ps_ready)

            def out_projection(g):
                pe.wait_ge(shifted, g * (B * C) + B * C)
                for t in range(B):
                    tile = slice(t * P, (t + 1) * P)
                    for c in range(C):
                        if t == 0:
                            pe.wait_ge(oT_hi_ready, g * C + c + 1)
                        last = passes(score_ps[t // 2][:, t % 2 * D:(t % 2 + 1) * D], oT_hi[:, c, tile], oT_lo[:, c, tile],
                                      wo_hi[:, c, :], wo_lo[:, c, :], c == 0, c == C - 1,
                                      w_lo_ready=(oT_ready, g * C + c + 1) if t == 0 else None)
                    if t % 2:
                        last.then_inc(wo_ps_ready, 1)

            def f_transposed(g):
                transposes(trans_ps, norm, x1n_ready, g * B, fT_ps_ready)

            def hidden(e, f):
                if f == 0:
                    pe.wait_ge(w_split, e * 2 + 1)
                if f < 2:
                    pe.wait_ge(final_done, e * B + B - 1 + f)
                if f >= 2:
                    pe.wait_ge(gelu_done, e * FC + f - 1)
                chunk = slice(f * P, (f + 1) * P)
                for c in range(C):
                    if f == 0:
                        pe.wait_ge(fT_hi_ready, e * C + c + 1)
                    last = passes(hid_ps[f % 2][:, :], w1_hi[:, c, chunk], w1_lo[:, c, chunk],
                                  fT_hi[:, c, :], fT_lo[:, c, :], c == 0, c == C - 1,
                                  m_lo_ready=(fT_ready, e * C + c + 1) if f == 0 else None)
                last.then_inc(h_ps_ready, 1)

            def ffn_out(e, t, start, end, banks=y_ps):
                if t == 0 and start == 0:
                    pe.wait_ge(w_split, e * 2 + 2)
                if banks is y_ps and start == 0:
                    if t < 2:
                        pe.wait_ge(gelu_done, e * FC + FC - 1 + t)
                    else:
                        pe.wait_ge(final_done, e * B + B + t - 1)
                tile = slice(t * P, (t + 1) * P)
                for f in range(start, end):
                    if t == 0:
                        pe.wait_ge(h_ready, e * FC + f + 1)
                    last = passes(banks[t], hT_hi[:, f, tile], hT_lo[:, f, tile],
                                  w2_hi[:, f, :], w2_lo[:, f, :], f == 0, f == FC - 1)
                if end == FC:
                    last.then_inc(y_ps_ready, 1)

            keys_product()
            x_transposed(0)
            context_transposed()
            pe.wait_ge(wq_ready, 1)
            queries(0, score_ps, False)
            values_product(0)
            pe.wait_ge(keys_hi_ready, 2)
            pe.wait_ge(keys_lo_ready, 2)
            scores(0, 0, score_ps, 2)
            scores(0, 1, hid_ps, 2)
            values_product(1)
            scores(0, 2, score_ps, 2)
            prob_transposed(0, 0)
            scores(0, 3, hid_ps, 2)
            prob_transposed(0, 1)
            pe.wait_ge(vals_ready, 2)
            weighted_values(0, 0)
            prob_transposed(0, 2)
            weighted_values(0, 1)
            pe.wait_ge(shifted, 3 * C)
            x_transposed(1, score_ps)
            weighted_values(0, 2)
            prob_transposed(0, 3)
            pe.wait_ge(shifted, 4 * C)
            queries(1, hid_ps, False, range(1))
            weighted_values(0, 3)
            o_transposed(0)
            queries(1, hid_ps, False, range(1, C))
            pe.wait_ge(wo_ready, 1)
            out_projection(0)
            f_transposed(0)

            def iteration(e, g, more):
                scores(g, 0)
                hidden(e, 0)
                hidden(e, 1)
                hidden(e, 2)
                scores(g, 1)
                for f in range(3, FC):
                    hidden(e, f)
                scores(g, 2)
                ffn_out(e, 0, 0, 6)
                ffn_out(e, 1, 0, 2)
                ffn_out(e, 0, 6, FC)
                ffn_out(e, 1, 2, 4)
                prob_transposed(g, 0)
                ffn_out(e, 1, 4, 6)
                prob_transposed(g, 1)
                weighted_values(g, 0)
                scores(g, 3)
                prob_transposed(g, 2)
                weighted_values(g, 1)
                weighted_values(g, 2)
                prob_transposed(g, 3)
                ffn_out(e, 1, 6, FC)
                ffn_out(e, 2, 0, 2)
                weighted_values(g, 3)
                ffn_out(e, 2, 2, 4)
                o_transposed(g)
                ffn_out(e, 2, 4, FC)
                if more:
                    x_transposed(g + 1)
                out_projection(g)
                ffn_out(e, 3, 0, 4)
                if more:
                    queries(g + 1)
                ffn_out(e, 3, 4, FC)
                f_transposed(g)

            with pe.Fori(0, E - 2) as i:
                iteration(i, i + 1, True)
            iteration(E - 2, E - 1, False)
            for f in range(FC):
                hidden(E - 1, f)
            for t, start, end in ((0, 0, 6), (1, 0, 6), (0, 6, FC), (1, 6, FC), (2, 0, FC), (3, 0, FC)):
                ffn_out(E - 1, t, start, end, y_last_ps)

        @block.scalar
        def _(act):
            activation = nc.scalar.activation
            for c in range(C):
                act.wait_ge(ctx_ps_ready, c + 1)
                activation(ctxG[:, c, :], score_ps[c][:, 0:B * K], ACT.Copy).then_inc(ctx_sb_ready, 1)

            def context_out():
                act.wait_ge(ctx_ps_ready, C + 1)
                for c in range(C):
                    last = activation(ctxT[:, c, :, :], trans_ps[c][:, :].rearrange("p (b k) -> p b k", b=B), ACT.Copy)
                last.then_inc(ctx_sb_ready, 1)

            def keys_high(heads):
                for h in heads:
                    last = activation(keys_hi[:, :, :, h, :], kT[:, :, :, :].rearrange("p c b k -> p b c k"),
                                      ACT.Copy, scale=head_of[:, h:h + 1])
                return last

            def values_out(half):
                act.wait_ge(kv_ps_ready, C + half + 1)
                act.wait_ge(vals_ones_ready, 1)
                for side in range(2):
                    rows = slice(side * K, (side + 1) * K)
                    dst = vals[rows, 2 * half:2 * half + 2, 0:PAIRS * PW].rearrange("p b (j n) -> p b j n", n=PW)
                    src = attn_ps[half][rows, :].rearrange("p (b j n) -> p b j n", b=2, n=2 * HD)
                    cols = slice(side * HD, (side + 1) * HD)
                    last = activation(dst[:, :, :, cols], src[:, :, :, cols], ACT.Copy, scale=wcol[rows, 0:1])
                last.then_inc(vals_scaled, 1)

            def x_hi(g, bank=attn_ps):
                for c in range(C):
                    act.wait_ge(xT_ps_ready, g * C + c + 1)
                    activation(xT_hi[:, c, :], bank[c][:, :], ACT.Copy).then_inc(xT_hi_ready, 1)

            def q_hi(g, bank=score_ps):
                for c in range(C):
                    act.wait_ge(q_ps_ready, g * C + c + 1)
                    activation(qT_hi[:, c, :], bank[c][:, :], ACT.Identity, bias=bq_sb[:, c:c + 1]).then_inc(q_hi_ready, 1)

            def exps(g, t):
                act.wait_ge(shifted, g * (B * C) + t * C + C)
                activation(prob[:, t % 2, :], prob[:, t % 2, :], ACT.Exp).then_inc(p_ready, 1)

            def prob_out(g, t):
                if t >= 2:
                    act.wait_ge(pv_ready, g * B + t - 1)
                for c in range(C):
                    act.wait_ge(pT_ps_ready, g * (B * C) + t * C + c + 1)
                    activation(probT[:, t % 2, c * (PAIRS // C):(c + 1) * (PAIRS // C), :],
                               trans_ps[c][:, :].rearrange("p (j q) -> p j q", q=P), ACT.Copy).then_inc(pT_ready, 1)

            def o_hi(g):
                for c in range(C):
                    act.wait_ge(oT_ps_ready, g * C + c + 1)
                    activation(oT_hi[:, c, :], trans_ps[c][:, :], ACT.Copy).then_inc(oT_hi_ready, 1)

            def f_hi(g):
                for c in range(C):
                    act.wait_ge(fT_ps_ready, g * C + c + 1)
                    activation(fT_hi[:, c, :], trans_ps[c][:, :], ACT.Copy).then_inc(fT_hi_ready, 1)

            def gelu(e, f):
                act.wait_ge(h_ps_ready, e * FC + f + 1)
                if f >= 2:
                    act.wait_ge(h_ready, e * FC + f - 1)
                activation(hid[:, f % 2, :], hid_ps[f % 2][:, :], ACT.Gelu,
                           bias=b1_bias(e, f)).then_inc(gelu_done, 1)

            def b1_bias(e, f):
                return b1_sb[:, bass.ds(e, 1), f]

            def h_hi(e, f):
                act.wait_ge(gelu_done, e * FC + f + 1)
                activation(hT_hi[:, f, :], hid[:, f % 2, :], ACT.Copy).then_inc(h_hi_ready, 1)

            act.wait_ge(kT_ready, 1)
            activation(kT_hi, kT, ACT.Copy).then_inc(kT_hi_ready, 1)
            x_hi(0)
            context_out()
            keys_high(range(0, 2))
            act.wait_ge(wq_loaded, 32)
            q_hi(0)
            keys_high(range(2, POOL_HI_HEAD)).then_inc(keys_hi_ready, 1)
            act.wait_ge(consts_loaded, 16 * 4)
            activation(gate[:, :], gates[:, :], ACT.Tanh).then_inc(gate_ready, 1)
            values_out(0)
            exps(0, 0)
            values_out(1)
            exps(0, 1)
            prob_out(0, 0)
            prob_out(0, 1)
            exps(0, 2)
            prob_out(0, 2)
            exps(0, 3)
            x_hi(1, score_ps)
            prob_out(0, 3)
            o_hi(0)
            act.wait_ge(wo_ps_ready, 2)
            q_hi(1, hid_ps)
            f_hi(0)

            def iteration(e, g, more):
                nc.scalar.preload_act_table(ACT.Gelu)
                for f in range(FC):
                    gelu(e, f)
                    h_hi(e, f)
                nc.scalar.preload_act_table(ACT.Exp)
                exps(g, 0)
                exps(g, 1)
                prob_out(g, 0)
                prob_out(g, 1)
                exps(g, 2)
                prob_out(g, 2)
                exps(g, 3)
                prob_out(g, 3)
                o_hi(g)
                if more:
                    x_hi(g + 1)
                    q_hi(g + 1)
                f_hi(g)

            with act.Fori(0, E - 2) as i:
                iteration(i, i + 1, True)
            iteration(E - 2, E - 1, False)
            nc.scalar.preload_act_table(ACT.Gelu)
            for f in range(FC):
                gelu(E - 1, f)
                h_hi(E - 1, f)

        @block.vector
        def _(dve):
            v = nc.vector
            self_count = [0]

            def done(ins):
                self_count[0] += 1
                ins.then_inc(dve_self, 1)
                dve.wait_ge(dve_self, self_count[0])

            dve.sem_inc(final_done, B)
            dve.wait_ge(mask_loaded, 48)
            v.tensor_scalar(mcol[:, :], mcol_i[:, :], 0.0, None, ALU.not_equal).then_inc(mask_ready, 1)
            done(v.tensor_scalar(mrow, mrow_i[:, :], 0.0, None, ALU.not_equal))
            dve.wait_ge(pool_const, 5)
            dve.wait_ge(mask_ready, 1)
            done(v.tensor_tensor(gdiag, ident[0:K, 0:K], mrow, ALU.mult))
            dve.wait_ge(count_ps_ready, 1)
            done(v.scalar_tensor_tensor(first[:, :], attn_ps[0][0:K, 0:1], 1.0, mcol[0:K, :], ALU.is_equal, ALU.mult))
            v.scalar_tensor_tensor(wcol[:, :], attn_ps[1][:, 0:1], 0.0, mcol[:, :], ALU.is_equal, ALU.add).then_inc(wcol_ready, 1)
            done(v.tensor_scalar(mrow, mrow, -1.0, 1.0, ALU.mult, ALU.add))
            v.scalar_tensor_tensor(gsel, mrow, first[:, 0:1], gdiag, ALU.mult, ALU.add).then_inc(gsel_ready, 1)

            def stats(g, n, half):
                xg = group(g)
                done = g * 4 + half * 2
                alone(dve)
                for t in (half * 2, half * 2 + 1):
                    last = v.bn_stats(stat6[:, t, :], xg[:, t, :])
                last.then_inc(stats_done[n], 1)
                dve.wait_ge(stats_done[n], done + 1)
                alone(dve)
                for t in (half * 2, half * 2 + 1):
                    last = v.bn_aggr(stat2[:, n, t, :], stat6[:, t, :])
                last.then_inc(stats_done[n], 1)
                dve.wait_ge(stats_done[n], done + 2)
                v.tensor_scalar(var_eps[:, n, half * 2:half * 2 + 2], stat2[:, n, half * 2:half * 2 + 2, 1], EPS, None,
                                ALU.add).then_inc((ln1_var, ln2_var)[n], 1)

            def scaled(g, n):
                xg = group(g)
                for t in range(B):
                    if t % 2 == 0:
                        dve.wait_ge((rstd1_ready, rstd2_ready)[n], g * 2 + t // 2 + 1)
                    v.tensor_scalar(norm[:, t, :], xg[:, t, :], stat2[:, n, t, 0:1], rstd[:, n, t:t + 1],
                                    ALU.subtract, ALU.mult).then_inc((xn_ready, x1n_ready)[n], 1)

            stats_done = [sem("stats1_done"), sem("stats2_done")]

            def keys_low(heads):
                for h in heads:
                    last = v.tensor_scalar(keys_lo[:, :, :, h, :], kT_lo[:, :, :, :].bitcast(F32).rearrange("p c b k -> p b c k"),
                                           head_of[:, h:h + 1], None, ALU.mult)
                return last

            def lo_part(lo, hi, ps, hi_ready, signal, g):
                for c in range(C):
                    dve.wait_ge(hi_ready, g * C + c + 1)
                    v.tensor_tensor(lo[:, c, :], ps[c][:, :], hi[:, c, :].bitcast(F32), ALU.subtract).then_inc(signal, 1)

            def q_lo(g, bank=score_ps):
                for c in range(C):
                    dve.wait_ge(q_hi_ready, g * C + c + 1)
                    v.scalar_tensor_tensor(qT_lo[:, c, :], bank[c][:, :], bq_sb[:, c:c + 1],
                                           qT_hi[:, c, :].bitcast(F32), ALU.add, ALU.subtract).then_inc(q_ready, 1)

            max_done = sem("max_done")
            rden_done = sem("rden_done")

            def shift(g, t, bank=score_ps):
                if t >= 2:
                    dve.wait_ge(pT_ps_ready, g * (B * C) + (t - 1) * C)
                for c in range(C):
                    dve.wait_ge(s_ps_ready, g * (B * C) + t * C + c + 1)
                    v.tensor_reduce(smax[:, t % 2, c * HG:(c + 1) * HG],
                                    bank[c][:, :].rearrange("p (h k) -> p h k", k=K), AX_X, ALU.max).then_inc(max_done, 1)
                for c in range(C):
                    dve.wait_ge(max_done, g * (B * C) + t * C + c + 1)
                    v.tensor_tensor(prob[:, t % 2, c * TOK:(c + 1) * TOK].rearrange("p (h k) -> p h k", k=K),
                                    bank[c][:, :].rearrange("p (h k) -> p h k", k=K),
                                    smax[:, t % 2, c * HG:(c + 1) * HG].unsqueeze(2).to_broadcast([P, HG, K]),
                                    ALU.subtract).then_inc(shifted, 1)

            def normalise(g, t):
                if t >= 2:
                    dve.wait_ge(o_ready, g * B + t - 1)
                dve.wait_ge(pv_ready, g * B + t + 1)
                pairs = attn_ps[t % 2][:, 0:PAIRS * PW].rearrange("p (j n) -> p j n", n=PW)
                v.reciprocal(rden[:, t % 2, :].rearrange("p (j a) -> p j a", a=2), pairs[:, :, 2 * HD:PW]).then_inc(rden_done, 1)
                dve.wait_ge(rden_done, g * B + t + 1)
                v.tensor_tensor(attn[:, t, :].rearrange("p (j a d) -> p j a d", a=2, d=HD),
                                pairs[:, :, 0:2 * HD].rearrange("p j (a d) -> p j a d", a=2),
                                rden[:, t % 2, :].rearrange("p (j a) -> p j a", a=2).unsqueeze(3).to_broadcast([P, PAIRS, 2, HD]),
                                ALU.mult).then_inc(o_ready, 1)

            def residual(g):
                dve.wait_ge(xb_ready, g + 1)
                xg = group(g).rearrange("p (h b) d -> p h (b d)", h=2)
                for n in range(2):
                    dve.wait_ge(wo_ps_ready, g * 2 + n + 1)
                    v.scalar_tensor_tensor(xg[:, n, :], score_ps[n][:, :], gate[:, 0:1], xg[:, n, :],
                                           ALU.mult, ALU.add).then_inc(x1_ready, 1)
                    dve.wait_ge(x1_ready, g * 2 + n + 1)
                    stats(g, 1, n)

            def h_lo(e, f):
                dve.wait_ge(h_hi_ready, e * FC + f + 1)
                v.tensor_tensor(hT_lo[:, f, :], hid[:, f % 2, :], hT_hi[:, f, :].bitcast(F32), ALU.subtract).then_inc(h_ready, 1)

            def final(e, t, banks=y_ps):
                if t == 0:
                    dve.wait_ge(x1b_ready, e + 1)
                dve.wait_ge(y_ps_ready, e * B + t + 1)
                xg = group(e)
                v.scalar_tensor_tensor(xg[:, t, :], banks[t], gate[:, 1:2], xg[:, t, :],
                                       ALU.mult, ALU.add).then_inc(final_done, 1)

            def x_scaled(g):
                scaled(g, 0)

            def x_lo(g, bank=attn_ps):
                lo_part(xT_lo, xT_hi, bank, xT_hi_ready, xT_ready, g)

            def o_lo(g):
                lo_part(oT_lo, oT_hi, trans_ps, oT_hi_ready, oT_ready, g)

            def f_lo(g):
                lo_part(fT_lo, fT_hi, trans_ps, fT_hi_ready, fT_ready, g)

            dve.wait_ge(x0_loaded, 16)
            stats(0, 0, 0)
            stats(0, 0, 1)
            scaled(0, 0)
            dve.wait_ge(vals_zero, 2)
            dve.wait_ge(wcol_ready, 1)
            for side in range(2):
                rows = slice(side * K, (side + 1) * K)
                dst = vals[rows, :, 0:PAIRS * PW].rearrange("p b (j n) -> p b j n", n=PW)
                last = v.tensor_scalar(dst[:, :, :, 2 * HD + side], ones[rows, 0:B * PAIRS].rearrange("p (b j) -> p b j", b=B),
                                       wcol[rows, 0:1], None, ALU.mult)
            last.then_inc(vals_ones_ready, 1)
            dve.wait_ge(wv_loaded, 32)
            for side in range(2):
                rows, cols = slice(side * K, (side + 1) * K), slice(side * HD, (side + 1) * HD)
                dst, src = (a[rows, :].rearrange("p (j n) -> p j n", n=2 * HD)[:, :, cols] for a in (bv_w, bv_sb))
                last = v.tensor_scalar(dst, src, wcol[rows, 0:1], None, ALU.mult)
            last.then_inc(bv_ready, 1)
            dve.wait_ge(wk_loaded, 32)
            for c in range(C):
                dve.wait_ge(kv_ps_ready, c + 1)
                last = v.tensor_scalar(kT[:, c, :, :], hid_ps[c][:, 0:B * K].rearrange("p (b k) -> p b k", b=B),
                                       bk_sb[:, c:c + 1], SCALE, ALU.add, ALU.mult)
            last.then_inc(kT_ready, 1)
            dve.wait_ge(kT_hi_ready, 1)
            v.tensor_tensor(kT_lo, kT, kT_hi.bitcast(F32), ALU.subtract).then_inc(kT_lo_ready, 1)
            x_lo(0)
            dve.wait_ge(kT_lo_ready, 1)
            keys_low(range(POOL_LO_HEAD)).then_inc(keys_lo_ready, 1)
            dve.wait_ge(wq_loaded, 32)
            q_lo(0)
            dve.wait_ge(x1_loaded, 16)
            stats(1, 0, 0)
            shift(0, 0)
            stats(1, 0, 1)
            dve.wait_ge(kv_ps_ready, C + 2)
            dve.wait_ge(wo_ready, 1)
            shift(0, 1, hid_ps)
            shift(0, 2)
            x_scaled(1)
            shift(0, 3, hid_ps)
            normalise(0, 0)
            dve.wait_ge(gate_ready, 1)
            v.tensor_scalar(bo_g[:, :], bo_sb, gate[:, 0:1], None, ALU.mult).then_inc(bo_ready, 1)
            normalise(0, 1)
            x_lo(1, score_ps)
            dve.wait_ge(bo_ready, 1)
            normalise(0, 2)
            normalise(0, 3)
            o_lo(0)
            residual(0)
            scaled(0, 1)
            q_lo(1, hid_ps)
            f_lo(0)
            dve.wait_ge(x_loaded, 16)

            def iteration(e, g, more):
                shift(g, 0)
                h_lo(e, 0)
                h_lo(e, 1)
                shift(g, 1)
                for f in range(2, FC):
                    h_lo(e, f)
                final(e, 0)
                shift(g, 2)
                normalise(g, 0)
                if more:
                    stats(g + 1, 0, 0)
                shift(g, 3)
                if more:
                    stats(g + 1, 0, 1)
                normalise(g, 1)
                normalise(g, 2)
                if more:
                    x_scaled(g + 1)
                final(e, 1)
                normalise(g, 3)
                o_lo(g)
                final(e, 2)
                if more:
                    x_lo(g + 1)
                residual(g)
                scaled(g, 1)
                if more:
                    q_lo(g + 1)
                final(e, 3)
                f_lo(g)

            with dve.Fori(0, E - 2) as i:
                iteration(i, i + 1, True)
            iteration(E - 2, E - 1, False)
            for f in range(FC):
                h_lo(E - 1, f)
            for t in range(B):
                final(E - 1, t, y_last_ps)


def kernel(x, ctx_1024, mask_1xS2_if1, g_xattn, g_ffn, L0_xattn_Wq, L0_xattn_bq, L0_xattn_Wk, L0_xattn_bk,
           L0_xattn_Wv, L0_xattn_bv, L0_xattn_Wo, L0_xattn_bo, L0_ffn_w1, L0_ffn_b1, L0_ffn_w2, L0_ffn_b2):
    import numpy as np
    import concourse.bacc as bacc
    from concourse.bass_utils import run_bass_kernel_spmd

    def halves(w):
        return np.ascontiguousarray(np.asarray(w).reshape(C, P, -1).transpose(1, 0, 2))

    def column(b):
        return np.ascontiguousarray(np.asarray(b).reshape(C, P).T)

    def row(b):
        return np.ascontiguousarray(np.asarray(b).reshape(1, -1))

    arrays = {
        "x": np.ascontiguousarray(np.asarray(x).reshape(B, E, P, D).transpose(1, 2, 0, 3)).reshape(E, P, B * D),
        "ctx": np.ascontiguousarray(np.asarray(ctx_1024).transpose(1, 0, 2)),
        "mask": np.ascontiguousarray(np.asarray(mask_1xS2_if1)),
        "g_x": row(g_xattn), "g_f": row(g_ffn),
        "wq": halves(L0_xattn_Wq), "bq": column(L0_xattn_bq),
        "wk": halves(L0_xattn_Wk), "bk": column(L0_xattn_bk),
        "wv": halves(L0_xattn_Wv), "bv": row(L0_xattn_bv),
        "wo": halves(L0_xattn_Wo), "bo": row(L0_xattn_bo),
        "w1": np.ascontiguousarray(np.asarray(L0_ffn_w1).reshape(E, F, C, P).transpose(0, 3, 2, 1)).reshape(E, P, C * F),
        "b1": np.ascontiguousarray(np.asarray(L0_ffn_b1).reshape(E, FC, P).transpose(2, 0, 1)),
        "w2": np.ascontiguousarray(np.asarray(L0_ffn_w2).reshape(E, D, FC, P).transpose(0, 3, 2, 1)).reshape(E, P, FC * D),
        "b2": np.ascontiguousarray(np.asarray(L0_ffn_b2)),
    }
    nc = bacc.Bacc("TRN2", target_bir_lowering=False, num_devices=1)
    feeds = {f"in_{n}": a for n, a in arrays.items()}
    args = [nc.dram_tensor(n, a.shape, mybir.dt.from_np(a.dtype), kind="ExternalInput").ap() for n, a in feeds.items()]
    out = nc.dram_tensor("out", (E, P, B * D), F32, kind="ExternalOutput").ap()
    build(nc, *args, out)
    r = run_bass_kernel_spmd(nc, [feeds], core_ids=[0])
    got = r.results[0]["out"].reshape(E, P, B, D).transpose(2, 0, 1, 3).reshape(B, S, D)
    return np.ascontiguousarray(got)
```

```python
from contextlib import ExitStack

import concourse.bass as bass
from concourse import mybir

F32 = mybir.dt.float32
F32R = mybir.dt.float32r
I32 = mybir.dt.int32
ALU = mybir.AluOpType
ACT = mybir.ActivationFunctionType
AX_X = mybir.AxisListType.X

P = 128
D = 256
C = D // P
B = 4
S = 1024
E = S // P
TOK = B * P
F = 1024
FC = F // P
H = 16
HD = D // H
K = 64
HG = H // C
PAIRS = H // 2
PW = 2 * HD + 2
PVN = 96
EPS = 1e-5
POOL_HI_HEAD, POOL_LO_HEAD = 3, 6
SCALE = 0.25


def build(nc, x, ctx, mask, g_x, g_f, wq, bq, wk, bk, wv, bv, wo, bo, w1, b1, w2, b2, out):
    stack = ExitStack()
    with stack:
        def sb(name, shape, dt=F32):
            return stack.enter_context(nc.sbuf_tensor(name, shape, dt))

        def sem(name):
            return stack.enter_context(nc.semaphore(name))

        xs = sb("xs", [P, E * B * D])
        attn = sb("attn", [P, B, D])
        norm = sb("norm", [P, B, D])
        xT_hi = sb("xT_hi", [P, C, TOK], F32R)
        xT_lo = sb("xT_lo", [P, C, TOK], F32R)
        fT_hi = sb("fT_hi", [P, C, TOK], F32R)
        fT_lo = sb("fT_lo", [P, C, TOK], F32R)
        qT = sb("qT", [P, C * 2, TOK], F32R)
        oT_hi, oT_lo = qT[:, 0:C, :], qT[:, C:2 * C, :]
        prob = sb("prob", [P, 2, H * K])
        probT = sb("probT", [P, 2, PAIRS, P])
        hid = sb("hid", [P, 2, TOK])
        hT_hi = sb("hT_hi", [P, FC, TOK], F32R)
        hT_lo = sb("hT_lo", [P, FC, TOK], F32R)
        w_raw = sb("w_raw", [P, C * F])
        w1_hi = sb("w1_hi", [P, C, F], F32R)
        w1_lo = sb("w1_lo", [P, C, F], F32R)
        w2_hi = sb("w2_hi", [P, FC, D], F32R)
        w2_lo = sb("w2_lo", [P, FC, D], F32R)
        wq_hi = sb("wq_hi", [P, C, D], F32R)
        wq_lo = sb("wq_lo", [P, C, D], F32R)
        wo_hi = sb("wo_hi", [P, C, D], F32R)
        wo_lo = sb("wo_lo", [P, C, D], F32R)
        keys_hi = sb("keys_hi", [P, B, C, HG, K], F32R)
        keys_lo = sb("keys_lo", [P, B, C, HG, K], F32R)
        vals = sb("vals", [P, B, (PAIRS - 1) * PW + PVN])
        ident = sb("ident", [P, P])
        b1_sb = sb("b1_sb", [P, E, FC])
        b2_sb = sb("b2_sb", [P, D])
        b2_g = sb("b2_g", [P, D])
        bo_g = sb("bo_g", [P, D])
        bq_sb = sb("bq_sb", [P, C])
        bk_sb = sb("bk_sb", [P, C])
        gates = sb("gates", [P, 2])
        gate = sb("gate", [P, 2])
        head_of = sb("head_of", [P, HG])
        twin_of = sb("twin_of", [P, HG // 2])
        minus_half = sb("minus_half", [P, B])
        stat6 = sb("stat6", [P, B, 6])
        stat2 = sb("stat2", [P, 2, B, 2])
        var_eps = sb("var_eps", [P, 2, B])
        rstd = sb("rstd", [P, 2, B])
        smax = sb("smax", [P, 2, H])
        rden = sb("rden", [P, 2, H])
        mcol_i = sb("mcol_i", [P, 1], I32)
        mcol = sb("mcol", [P, 1])
        wcol = sb("wcol", [P, 1])
        first = sb("first", [K, 1])
        w_set = prob[:, :, :].rearrange("p a (n c d) -> p (a n) c d", n=2, c=C)
        kT_hi = [hT_hi[:, 2 + side, :].rearrange("p (c b k) -> p c b k", c=C, b=B) for side in range(2)]
        kT_lo = hT_hi[:, 1, :].rearrange("p (c b k) -> p c b k", c=C, b=B)
        ctx_sb = probT[0:K, 0, :, :].rearrange("p j q -> p (j q)").rearrange("p (b d) -> p b d", b=B)
        ctxT = probT[:, 1, :, :].rearrange("p j q -> p (j q)").rearrange("p (c b k) -> p c b k", c=C, b=B)
        ctxG = hid[:, 0, :].rearrange("p (c n) -> p c n", c=C)
        kT = hid[:, 1, :].rearrange("p (c b k) -> p c b k", c=C, b=B)
        bv_sb = attn[:, 0, :]
        bv_w = attn[:, 1, :]
        bo_sb = attn[:, 2, :]
        small = attn[0:K, 3, :]
        mrow = small[:, 0:K]
        gsel = small[:, K:2 * K]
        gdiag = small[:, 2 * K:3 * K]
        mrow_i = sb("mrow_i", [K, K], I32)
        tri = sb("tri", [K, K])
        ones = sb("ones", [P, P])
        ident2 = sb("ident2", [K, 2, K])

        score_ps = [stack.enter_context(nc.psum_tensor(f"score_ps{i}", [P, TOK], F32)) for i in range(2)]
        trans_ps = [stack.enter_context(nc.psum_tensor(f"trans_ps{i}", [P, TOK], F32)) for i in range(2)]
        hid_ps = [stack.enter_context(nc.psum_tensor(f"hid_ps{i}", [P, TOK], F32)) for i in range(2)]
        attn_ps = [stack.enter_context(nc.psum_tensor(f"attn_ps{i}", [P, TOK], F32)) for i in range(2)]
        y_ps = [bank[:, 0:D] for bank in hid_ps] * 2
        y_last_ps = [bank[:, 0:D] for bank in score_ps + hid_ps]

        x0_loaded, x1_loaded, x_loaded, w_loaded, b2_loaded = sem("x0_loaded"), sem("x1_loaded"), sem("x_loaded"), sem("w_loaded"), sem("b2_loaded")
        mask_loaded, ctx_loaded, consts_loaded = sem("mask_loaded"), sem("ctx_loaded"), sem("consts_loaded")
        wk_loaded, wq_loaded, wv_loaded, wo_loaded = sem("wk_loaded"), sem("wq_loaded"), sem("wv_loaded"), sem("wo_loaded")
        stored = sem("stored")
        waited = sem("waited")
        pool_const, pool_self, dve_self = sem("pool_const"), sem("pool_self"), sem("dve_self")
        mask_ready, count_ps_ready, gsel_ready = sem("mask_ready"), sem("count_ps_ready"), sem("gsel_ready")
        ctx_ps_ready, ctx_sb_ready, kv_ps_ready = sem("ctx_ps_ready"), sem("ctx_sb_ready"), sem("kv_ps_ready")
        kT_ready, kT_hi_ready, kT_lo_ready = sem("kT_ready"), sem("kT_hi_ready"), sem("kT_lo_ready")
        keys_hi_ready, keys_lo_ready = sem("keys_hi_ready"), sem("keys_lo_ready")
        vals_zero, wcol_ready, vals_ones_ready, vals_scaled, bv_ready, vals_ready = sem("vals_zero"), sem("wcol_ready"), sem("vals_ones_ready"), sem("vals_scaled"), sem("bv_ready"), sem("vals_ready")
        gate_ready, bo_ready, wq_ready, wo_ready = sem("gate_ready"), sem("bo_ready"), sem("wq_ready"), sem("wo_ready")
        ln1_var, rstd1_ready, xn_ready, xb_ready = sem("ln1_var"), sem("rstd1_ready"), sem("xn_ready"), sem("xb_ready")
        xT_ps_ready, xT_hi_ready, xT_ready = sem("xT_ps_ready"), sem("xT_hi_ready"), sem("xT_ready")
        q_ps_ready, q_hi_ready, q_ready = sem("q_ps_ready"), sem("q_hi_ready"), sem("q_ready")
        s_ps_ready, shifted, p_ready = sem("s_ps_ready"), sem("shifted"), sem("p_ready")
        pT_ps_ready, pT_ready, pv_ready, o_ready = sem("pT_ps_ready"), sem("pT_ready"), sem("pv_ready"), sem("o_ready")
        oT_ps_ready, oT_hi_ready, oT_ready = sem("oT_ps_ready"), sem("oT_hi_ready"), sem("oT_ready")
        wo_ps_ready, x1_ready, ln2_var, rstd2_ready, x1n_ready, x1b_ready = sem("wo_ps_ready"), sem("x1_ready"), sem("ln2_var"), sem("rstd2_ready"), sem("x1n_ready"), sem("x1b_ready")
        fT_ps_ready, fT_hi_ready, fT_ready = sem("fT_ps_ready"), sem("fT_hi_ready"), sem("fT_ready")
        h_ps_ready, gelu_done, h_hi_ready, h_ready = sem("h_ps_ready"), sem("gelu_done"), sem("h_hi_ready"), sem("h_ready")
        y_ps_ready, final_done, w_split = sem("y_ps_ready"), sem("final_done"), sem("w_split")

        def group(g):
            return xs[:, bass.ds(g * (B * D), B * D)].rearrange("p (b d) -> p b d", b=B)

        def half_rows(side):
            return slice(side * P // 2, (side + 1) * P // 2)

        def keys_hi_part(half, h):
            two = slice(half * 2, half * 2 + 2)
            return (keys_hi[:, two, :, h, :], kT_hi[h // (HG // 2)][:, :, two, :].bitcast(F32).rearrange("p c b k -> p b c k"),
                    twin_of[:, h % (HG // 2):h % (HG // 2) + 1])

        def keys_lo_part(half, h):
            two = slice(half * 2, half * 2 + 2)
            return (keys_lo[:, two, :, h, :], kT_lo[:, :, two, :].bitcast(F32).rearrange("p c b k -> p b c k"),
                    head_of[:, h:h + 1])

        def alone(engine):
            engine.sem_inc(waited, 1)

        block = stack.enter_context(nc.Block())

        @block.sync
        def _(sp):
            def load_w(src, e):
                sp.dma_start(w_raw[:, :], src[bass.ds(e, 1), :, :].rearrange("e p n -> p (e n)")).then_inc(w_loaded, 16)

            def load_b2(e):
                sp.dma_start(b2_sb[:, :], b2[bass.ds(e, 1), :].to_broadcast([P, D])).then_inc(b2_loaded, 16)

            def store(e):
                sp.dma_start(out[bass.ds(e, 1), :, :].rearrange("e p n -> p (e n)"),
                             xs[:, bass.ds(e * (B * D), B * D)]).then_inc(stored, 16)

            sp.dma_start(mrow_i[:, :], mask.to_broadcast([K, K])).then_inc(mask_loaded, 16)
            for half in range(2):
                sp.dma_start(mcol_i[half * K:(half + 1) * K, :], mask.rearrange("o k -> k o")).then_inc(mask_loaded, 16)
            sp.dma_start(ctx_sb, ctx).then_inc(ctx_loaded, 16)
            sp.dma_start(xs[:, 0:B * D], x[0, :, :]).then_inc(x0_loaded, 16)
            sp.dma_start(w_set[:, 0, :, :], wk).then_inc(wk_loaded, 16)
            sp.dma_start(bk_sb[:, :], bk).then_inc(wk_loaded, 16)
            sp.dma_start(w_set[:, 1, :, :], wq).then_inc(wq_loaded, 16)
            sp.dma_start(bq_sb[:, :], bq).then_inc(wq_loaded, 16)
            sp.dma_start(w_set[:, 2, :, :], wv).then_inc(wv_loaded, 16)
            sp.dma_start(bv_sb, bv.to_broadcast([P, D])).then_inc(wv_loaded, 16)
            sp.dma_start(xs[:, B * D:2 * B * D], x[1, :, :]).then_inc(x1_loaded, 16)
            sp.dma_start(w_set[:, 3, :, :], wo).then_inc(wo_loaded, 16)
            sp.dma_start(bo_sb, bo.to_broadcast([P, D])).then_inc(consts_loaded, 16)
            sp.dma_start(gates[:, 0:1], g_x.to_broadcast([P, 1])).then_inc(consts_loaded, 16)
            sp.dma_start(gates[:, 1:2], g_f.to_broadcast([P, 1])).then_inc(consts_loaded, 16)
            sp.dma_start(b1_sb[:, :, :], b1).then_inc(consts_loaded, 16)
            load_w(w1, 0)
            load_b2(0)
            sp.dma_start(xs[:, 2 * B * D:E * B * D].rearrange("p (e n) -> p e n", e=E - 2),
                         x[2:E, :, :].rearrange("e p n -> p e n")).then_inc(x_loaded, 16)
            sp.wait_ge(w_split, 1)
            load_w(w2, 0)
            with sp.Fori(0, E - 1) as i:
                sp.wait_ge(w_split, i * 2 + 2)
                load_w(w1, i + 1)
                sp.wait_ge(x1b_ready, i + 1)
                load_b2(i + 1)
                sp.wait_ge(w_split, i * 2 + 3)
                load_w(w2, i + 1)
                sp.wait_ge(final_done, i * B + 2 * B)
                store(i)
            last = xs[:, (E - 1) * B * D:E * B * D]
            sp.wait_ge(final_done, E * B + B - 1)
            sp.dma_start(out[E - 1, :, 0:(B - 1) * D], last[:, 0:(B - 1) * D]).then_inc(stored, 16)
            sp.wait_ge(final_done, E * B + B)
            sp.dma_start(out[E - 1, :, (B - 1) * D:B * D], last[:, (B - 1) * D:B * D]).then_inc(stored, 16)
            sp.wait_ge(stored, (E + 1) * 16)

        @block.gpsimd
        def _(pool):
            self_count = [0]

            def done(ins):
                self_count[0] += 1
                ins.then_inc(pool_self, 1)
                pool.wait_ge(pool_self, self_count[0])

            gp = nc.gpsimd
            done(gp.memset(ident[:, :], 0.0))
            gp.affine_select(out=ident[:, :], in_=ident[:, :], compare_op=ALU.not_equal, fill=1.0, base=0,
                             pattern=[[-1, P]], channel_multiplier=1).then_inc(pool_const, 1)
            done(gp.memset(ident2[:, :, :], 0.0))
            gp.affine_select(out=ident2[:, :, :], in_=ident2[:, :, :], compare_op=ALU.not_equal, fill=1.0, base=0,
                             pattern=[[0, 2], [-1, K]], channel_multiplier=1).then_inc(pool_const, 1)
            done(gp.memset(tri[:, :], 1.0))
            gp.affine_select(out=tri[:, :], in_=tri[:, :], compare_op=ALU.is_ge, fill=0.0, base=0,
                             pattern=[[1, K]], channel_multiplier=-1).then_inc(pool_const, 1)
            gp.memset(ones[:, :], 1.0).then_inc(pool_const, 1)
            done(gp.memset(head_of[:, :], 1.0))
            done(gp.affine_select(out=head_of[:, :], in_=head_of[:, :], compare_op=ALU.is_ge, fill=0.0, base=0,
                                  pattern=[[-HD, HG]], channel_multiplier=1))
            gp.affine_select(out=head_of[:, :], in_=head_of[:, :], compare_op=ALU.is_ge, fill=0.0, base=HD - 1,
                             pattern=[[HD, HG]], channel_multiplier=-1).then_inc(pool_const, 1)
            pool.wait_ge(pool_const, 5)
            gp.tensor_tensor(twin_of[:, :], head_of[:, 0:HG // 2], head_of[:, HG // 2:HG], ALU.add).then_inc(pool_const, 1)
            gp.memset(minus_half[:, :], -0.5).then_inc(pool_const, 1)
            gp.memset(vals[:, :, :], 0.0).then_inc(vals_zero, 1)
            gp.memset(bv_w, 0.0).then_inc(vals_zero, 1)
            pool.wait_ge(pool_const, 7)

            def power(g, n):
                for half in range(2):
                    tiles = slice(half * 2, half * 2 + 2)
                    pool.wait_ge((ln1_var, ln2_var)[n], g * 2 + half + 1)
                    gp.tensor_tensor(rstd[:, n, tiles], var_eps[:, n, tiles], minus_half[:, tiles],
                                     ALU.pow).then_inc((rstd1_ready, rstd2_ready)[n], 1)

            def add_bo(g):
                xg = group(g)
                pool.wait_ge(xn_ready, g * B + B)
                alone(pool)
                for t in range(B):
                    last = gp.tensor_tensor(xg[:, t, :], xg[:, t, :], bo_g[:, :], ALU.add)
                last.then_inc(xb_ready, 1)

            def split(hi, lo, count):
                alone(pool)
                for n in range(4):
                    part = slice(n * 512, (n + 1) * 512)
                    gp.tensor_scalar(hi[:, part], w_raw[:, part], 1.0, 0.0, ALU.mult, ALU.add).then_inc(hi_parts, 1)
                for n in range(4):
                    part = slice(n * 512, (n + 1) * 512)
                    pool.wait_ge(hi_parts, count * 4 + n + 1)
                    last = gp.tensor_tensor(lo[:, part], w_raw[:, part], hi[:, part].bitcast(F32), ALU.subtract)
                last.then_inc(w_split, 1)

            hi_parts = sem("hi_parts")

            def split_w1(e):
                pool.wait_ge(w_loaded, e * 32 + 16)
                split(w1_hi[:, :, :].rearrange("p c f -> p (c f)"), w1_lo[:, :, :].rearrange("p c f -> p (c f)"), e * 2)

            def split_w2(e):
                pool.wait_ge(w_loaded, e * 32 + 32)
                pool.wait_ge(final_done, e * B + B)
                split(w2_hi[:, :, :].rearrange("p c f -> p (c f)"), w2_lo[:, :, :].rearrange("p c f -> p (c f)"), e * 2 + 1)

            def add_b2(g):
                pool.wait_ge(b2_loaded, g * 16 + 16)
                alone(pool)
                gp.tensor_scalar(b2_g[:, :], b2_sb[:, :], gate[:, 1:2], 0.0, ALU.mult, ALU.add).then_inc(b2g_ready, 1)
                pool.wait_ge(b2g_ready, g + 1)
                pool.wait_ge(x1n_ready, g * B + B)
                alone(pool)
                xg = group(g)
                for t in range(B):
                    last = gp.tensor_tensor(xg[:, t, :], xg[:, t, :], b2_g[:, :], ALU.add)
                last.then_inc(x1b_ready, 1)

            b2g_ready = sem("b2g_ready")

            def split_set(hi, lo, n, loaded, parts, signal):
                pool.wait_ge(*loaded)
                whole = w_set[:, n, :, :]
                gp.tensor_scalar(hi[:, :, :], whole, 1.0, 0.0, ALU.mult, ALU.add).then_inc(parts, 1)
                pool.wait_ge(parts, 1)
                gp.tensor_tensor(lo[:, :, :], whole, hi[:, :, :].bitcast(F32), ALU.subtract).then_inc(signal, 1)

            def values_bias(half):
                pool.wait_ge(vals_scaled, half + 1)
                alone(pool)
                bias = bv_w.rearrange("p (j n) -> p j n", n=2 * HD)
                for b in (half * 2, half * 2 + 1):
                    dst = vals[:, b, 0:PAIRS * PW].rearrange("p (j n) -> p j n", n=PW)[:, :, 0:2 * HD]
                    last = gp.tensor_tensor(dst, dst, bias, ALU.add)
                last.then_inc(vals_ready, 1)

            power(0, 0)
            split_set(wq_hi, wq_lo, 1, (wq_loaded, 32), sem("wq_hi_ready"), wq_ready)
            pool.wait_ge(kT_hi_ready, 4)
            alone(pool)
            for h in range(POOL_HI_HEAD, HG):
                last = gp.tensor_scalar(*keys_hi_part(0, h), 0.0, ALU.mult, ALU.add)
            last.then_inc(keys_hi_ready, 1)
            pool.wait_ge(kT_lo_ready, 1)
            alone(pool)
            for h in range(POOL_LO_HEAD, HG):
                last = gp.tensor_scalar(*keys_lo_part(0, h), 0.0, ALU.mult, ALU.add)
            last.then_inc(keys_lo_ready, 1)
            for h in range(HG):
                last = gp.tensor_scalar(*keys_lo_part(1, h), 0.0, ALU.mult, ALU.add)
            last.then_inc(keys_lo_ready, 1)
            split_set(wo_hi, wo_lo, 3, (wo_loaded, 16), sem("wo_hi_ready"), wo_ready)
            pool.wait_ge(bv_ready, 1)
            values_bias(0)
            values_bias(1)
            split_w1(0)
            power(1, 0)
            pool.wait_ge(bo_ready, 1)
            add_bo(0)
            power(0, 1)
            add_bo(1)
            add_b2(0)

            def iteration(e, g, more):
                split_w2(e)
                if more:
                    power(g + 1, 0)
                pool.wait_ge(h_ps_ready, e * FC + FC)
                split_w1(g)
                power(g, 1)
                if more:
                    add_bo(g + 1)
                add_b2(g)

            with pool.Fori(0, E - 2) as i:
                iteration(i, i + 1, True)
            iteration(E - 2, E - 1, False)
            split_w2(E - 1)

        @block.tensor
        def _(pe):
            mm = nc.tensor.matmul

            def passes(o, w_hi, w_lo, m_hi, m_lo, start, stop, m_lo_ready=None, w_lo_ready=None):
                mm(o, w_hi, m_hi, start=start, stop=False)
                if m_lo_ready:
                    mm(o, w_lo, m_hi, start=False, stop=False)
                    pe.wait_ge(*m_lo_ready)
                    return mm(o, w_hi, m_lo, start=False, stop=stop)
                mm(o, w_hi, m_lo, start=False, stop=False)
                if w_lo_ready:
                    pe.wait_ge(*w_lo_ready)
                return mm(o, w_lo, m_hi, start=False, stop=stop)

            pe.wait_ge(pool_const, 4)
            pe.wait_ge(mask_ready, 1)
            mm(attn_ps[0][0:K, 0:1], tri[:, :], mcol[0:K, :], start=True, stop=True)
            mm(attn_ps[1][:, 0:1], ones[:, :], mcol[:, :], start=True, stop=True).then_inc(count_ps_ready, 1)
            pe.wait_ge(ctx_loaded, 16)
            pe.wait_ge(gsel_ready, 1)
            for c in range(C):
                for b in range(B):
                    last = mm(score_ps[c][:, b * K:(b + 1) * K], ctx_sb[:, b, c * P:(c + 1) * P],
                              gsel, start=True, stop=True)
                last.then_inc(ctx_ps_ready, 1)

            def context_transposed():
                for c in range(C):
                    for b in range(B):
                        last = mm(trans_ps[c][:, b * P:(b + 1) * P], ctx_sb[:, b, c * P:(c + 1) * P],
                                  ident2[:, :, :].rearrange("p a k -> p (a k)"), start=True, stop=True)
                last.then_inc(ctx_ps_ready, 1)

            def keys_product():
                pe.wait_ge(wk_loaded, 32)
                for m in range(C):
                    for c in range(C):
                        if m == 0:
                            pe.wait_ge(ctx_sb_ready, c + 1)
                        last = mm(hid_ps[m][:, 0:B * K], w_set[:, 0, c, m * P:(m + 1) * P], ctxG[:, c, :],
                                  start=(c == 0), stop=(c == C - 1))
                    last.then_inc(kv_ps_ready, 1)

            def values_product(half):
                pe.wait_ge(wv_loaded, 32)
                pe.wait_ge(ctx_sb_ready, C + 1)
                for b in range(2):
                    bank = attn_ps[half][:, b * D:(b + 1) * D]
                    for c in range(C):
                        last = mm(bank, ctxT[:, c, half * 2 + b, :], w_set[:, 2, c, :], start=(c == 0), stop=(c == C - 1))
                last.then_inc(kv_ps_ready, 1)

            def transposes(bank, src, ready, count, signal):
                for t in range(B):
                    pe.wait_ge(ready, count + t + 1)
                    for c in range(C):
                        last = nc.tensor.transpose(bank[c][:, t * P:(t + 1) * P], src[:, t, c * P:(c + 1) * P], ident[:, :])
                        if t == B - 1:
                            last.then_inc(signal, 1)

            def x_transposed(g):
                transposes(attn_ps, norm, xn_ready, g * B, xT_ps_ready)

            def queries(g, after_residual=True, chunks=range(C)):
                for m in chunks:
                    if after_residual:
                        pe.wait_ge(x1_ready, (g - 1) * C + m + 1)
                    for c in range(C):
                        if m == 0:
                            pe.wait_ge(xT_hi_ready, g * C + c + 1)
                        last = passes(score_ps[m][:, :], wq_hi[:, c, m * P:(m + 1) * P], wq_lo[:, c, m * P:(m + 1) * P],
                                      xT_hi[:, c, :], xT_lo[:, c, :], c == 0, c == C - 1,
                                      m_lo_ready=(xT_ready, g * C + c + 1) if m == 0 else None)
                    last.then_inc(q_ps_ready, 1)

            def scores(g, t, bank=score_ps, before=1):
                for c in range(C):
                    if t >= before:
                        pe.wait_ge(shifted, g * (B * C) + (t - before) * C + c + 1)
                    if t == 0:
                        pe.wait_ge(q_ready, g * (C * 2) + c * 2 + 2)
                    for side in range(2):
                        heads = slice(side * HG // 2, (side + 1) * HG // 2)
                        o = bank[c][:, side * TOK // 2:(side + 1) * TOK // 2]
                        q = qT[:, c * 2 + side, t * P:(t + 1) * P]
                        mm(o, q, keys_hi[:, t, c, heads, :].rearrange("p h k -> p (h k)"), start=True, stop=False)
                        last = mm(o, q, keys_lo[:, t, c, heads, :].rearrange("p h k -> p (h k)"), start=False, stop=True)
                    last.then_inc(s_ps_ready, 1)

            def prob_transposed(g, t):
                pe.wait_ge(p_ready, g * B + t + 1)
                for c in range(C):
                    if t > 0:
                        pe.wait_ge(pT_ready, g * (B * C) + (t - 1) * C + c + 1)
                    for j in range(PAIRS // C):
                        pair = c * (PAIRS // C) + j
                        last = nc.tensor.transpose(trans_ps[c][:, j * P:(j + 1) * P],
                                                   prob[:, t % 2, pair * P:(pair + 1) * P], ident[:, :])
                    last.then_inc(pT_ps_ready, 1)

            def weighted_values(g, t):
                pe.wait_ge(pT_ready, g * (B * C) + t * C + C)
                if t >= 2:
                    pe.wait_ge(o_ready, g * B + t - 1)
                for j in range(PAIRS):
                    last = mm(attn_ps[t % 2][:, j * PW:j * PW + PVN], probT[:, t % 2, j, :], vals[:, t, j * PW:j * PW + PVN],
                              start=True, stop=True)
                last.then_inc(pv_ready, 1)

            def o_transposed(g):
                transposes(trans_ps, attn, o_ready, g * B, oT_ps_ready)

            def out_projection(g):
                pe.wait_ge(shifted, g * (B * C) + B * C)
                for t in range(B):
                    tile = slice(t * P, (t + 1) * P)
                    for c in range(C):
                        if t == 0:
                            pe.wait_ge(oT_hi_ready, g * C + c + 1)
                        last = passes(score_ps[t // 2][:, t % 2 * D:(t % 2 + 1) * D], oT_hi[:, c, tile], oT_lo[:, c, tile],
                                      wo_hi[:, c, :], wo_lo[:, c, :], c == 0, c == C - 1,
                                      w_lo_ready=(oT_ready, g * C + c + 1) if t == 0 else None)
                    if t % 2:
                        last.then_inc(wo_ps_ready, 1)

            def f_transposed(g):
                transposes(trans_ps, norm, x1n_ready, g * B, fT_ps_ready)

            def hidden(e, f):
                if f == 0:
                    pe.wait_ge(w_split, e * 2 + 1)
                if f < 2:
                    pe.wait_ge(final_done, e * B + B - 1 + f)
                if f >= 2:
                    pe.wait_ge(gelu_done, e * FC + f - 1)
                chunk = slice(f * P, (f + 1) * P)
                for c in range(C):
                    if f == 0:
                        pe.wait_ge(fT_hi_ready, e * C + c + 1)
                    last = passes(hid_ps[f % 2][:, :], w1_hi[:, c, chunk], w1_lo[:, c, chunk],
                                  fT_hi[:, c, :], fT_lo[:, c, :], c == 0, c == C - 1,
                                  m_lo_ready=(fT_ready, e * C + c + 1) if f == 0 else None)
                last.then_inc(h_ps_ready, 1)

            def ffn_out(e, t, start, end, banks=y_ps):
                if t == 0 and start == 0:
                    pe.wait_ge(w_split, e * 2 + 2)
                if banks is y_ps and start == 0:
                    if t < 2:
                        pe.wait_ge(gelu_done, e * FC + FC - 1 + t)
                    else:
                        pe.wait_ge(final_done, e * B + B + t - 1)
                tile = slice(t * P, (t + 1) * P)
                for f in range(start, end):
                    if t == 0:
                        pe.wait_ge(h_ready, e * FC + f + 1)
                    last = passes(banks[t], hT_hi[:, f, tile], hT_lo[:, f, tile],
                                  w2_hi[:, f, :], w2_lo[:, f, :], f == 0, f == FC - 1)
                if end == FC:
                    last.then_inc(y_ps_ready, 1)

            keys_product()
            x_transposed(0)
            context_transposed()
            pe.wait_ge(wq_ready, 1)
            queries(0, False)
            values_product(0)
            pe.wait_ge(keys_hi_ready, 2)
            pe.wait_ge(keys_lo_ready, 2)
            scores(0, 0, score_ps, 2)
            scores(0, 1, hid_ps, 2)
            values_product(1)
            pe.wait_ge(keys_hi_ready, 3)
            pe.wait_ge(keys_lo_ready, 3)
            scores(0, 2, score_ps, 2)
            prob_transposed(0, 0)
            scores(0, 3, hid_ps, 2)
            prob_transposed(0, 1)
            pe.wait_ge(vals_ready, 2)
            weighted_values(0, 0)
            prob_transposed(0, 2)
            weighted_values(0, 1)
            prob_transposed(0, 3)
            weighted_values(0, 2)
            weighted_values(0, 3)
            o_transposed(0)
            x_transposed(1)
            pe.wait_ge(wo_ready, 1)
            out_projection(0)
            queries(1)
            f_transposed(0)

            def iteration(e, g, more):
                for f in range(3):
                    hidden(e, f)
                scores(g, 0)
                for f in range(3, 5):
                    hidden(e, f)
                scores(g, 1)
                for f in range(5, FC):
                    hidden(e, f)
                scores(g, 2)
                ffn_out(e, 0, 0, 6)
                ffn_out(e, 1, 0, 2)
                ffn_out(e, 0, 6, FC)
                ffn_out(e, 1, 2, 4)
                prob_transposed(g, 0)
                ffn_out(e, 1, 4, 5)
                prob_transposed(g, 1)
                weighted_values(g, 0)
                scores(g, 3)
                prob_transposed(g, 2)
                weighted_values(g, 1)
                weighted_values(g, 2)
                prob_transposed(g, 3)
                ffn_out(e, 1, 5, FC)
                weighted_values(g, 3)
                ffn_out(e, 2, 0, 2)
                o_transposed(g)
                ffn_out(e, 2, 2, 5)
                if more:
                    x_transposed(g + 1)
                out_projection(g)
                ffn_out(e, 2, 5, FC)
                if more:
                    queries(g + 1, chunks=range(1))
                ffn_out(e, 3, 0, 3)
                if more:
                    queries(g + 1, chunks=range(1, C))
                f_transposed(g)
                ffn_out(e, 3, 3, FC)

            with pe.Fori(0, E - 2) as i:
                iteration(i, i + 1, True)
            iteration(E - 2, E - 1, False)
            for f in range(FC):
                hidden(E - 1, f)
            for t, start, end in ((0, 0, 6), (1, 0, 6), (0, 6, FC), (1, 6, FC), (2, 0, FC), (3, 0, FC)):
                ffn_out(E - 1, t, start, end, y_last_ps)

        @block.scalar
        def _(act):
            activation = nc.scalar.activation
            for c in range(C):
                act.wait_ge(ctx_ps_ready, c + 1)
                activation(ctxG[:, c, :], score_ps[c][:, 0:B * K], ACT.Copy).then_inc(ctx_sb_ready, 1)

            def context_out():
                act.wait_ge(ctx_ps_ready, C + 1)
                for c in range(C):
                    last = activation(ctxT[:, c, :, :], trans_ps[c][:, :].rearrange("p (b k) -> p b k", b=B), ACT.Copy)
                last.then_inc(ctx_sb_ready, 1)

            def keys_high(half, heads):
                for h in heads:
                    block, rows, mine = keys_hi_part(half, h)
                    last = activation(block, rows, ACT.Copy, scale=mine)
                last.then_inc(keys_hi_ready, 1)

            def values_out(half):
                act.wait_ge(kv_ps_ready, C + half + 1)
                act.wait_ge(vals_ones_ready, 1)
                for side in range(2):
                    rows = slice(side * K, (side + 1) * K)
                    dst = vals[rows, 2 * half:2 * half + 2, 0:PAIRS * PW].rearrange("p b (j n) -> p b j n", n=PW)
                    src = attn_ps[half][rows, :].rearrange("p (b j n) -> p b j n", b=2, n=2 * HD)
                    cols = slice(side * HD, (side + 1) * HD)
                    last = activation(dst[:, :, :, cols], src[:, :, :, cols], ACT.Copy, scale=wcol[rows, 0:1])
                last.then_inc(vals_scaled, 1)

            def x_hi(g):
                for c in range(C):
                    act.wait_ge(xT_ps_ready, g * C + c + 1)
                    activation(xT_hi[:, c, :], attn_ps[c][:, :], ACT.Copy).then_inc(xT_hi_ready, 1)

            def q_hi(g):
                for c in range(C):
                    act.wait_ge(q_ps_ready, g * C + c + 1)
                    for side in range(2):
                        rows = half_rows(side)
                        activation(qT[rows, c * 2 + side, :], score_ps[c][rows, :], ACT.Identity,
                                   bias=bq_sb[rows, c:c + 1]).then_inc(q_hi_ready, 1)

            def exps(g, t):
                act.wait_ge(shifted, g * (B * C) + t * C + C)
                activation(prob[:, t % 2, :], prob[:, t % 2, :], ACT.Exp).then_inc(p_ready, 1)

            def prob_out(g, t):
                if t >= 2:
                    act.wait_ge(pv_ready, g * B + t - 1)
                for c in range(C):
                    act.wait_ge(pT_ps_ready, g * (B * C) + t * C + c + 1)
                    activation(probT[:, t % 2, c * (PAIRS // C):(c + 1) * (PAIRS // C), :],
                               trans_ps[c][:, :].rearrange("p (j q) -> p j q", q=P), ACT.Copy).then_inc(pT_ready, 1)

            def o_hi(g):
                for c in range(C):
                    act.wait_ge(oT_ps_ready, g * C + c + 1)
                    activation(oT_hi[:, c, :], trans_ps[c][:, :], ACT.Copy).then_inc(oT_hi_ready, 1)

            def f_hi(g):
                for c in range(C):
                    act.wait_ge(fT_ps_ready, g * C + c + 1)
                    activation(fT_hi[:, c, :], trans_ps[c][:, :], ACT.Copy).then_inc(fT_hi_ready, 1)

            def gelu(e, f):
                act.wait_ge(h_ps_ready, e * FC + f + 1)
                if f >= 2:
                    act.wait_ge(h_ready, e * FC + f - 1)
                activation(hid[:, f % 2, :], hid_ps[f % 2][:, :], ACT.Gelu,
                           bias=b1_bias(e, f)).then_inc(gelu_done, 1)

            def b1_bias(e, f):
                return b1_sb[:, bass.ds(e, 1), f]

            def h_hi(e, f):
                act.wait_ge(gelu_done, e * FC + f + 1)
                activation(hT_hi[:, f, :], hid[:, f % 2, :], ACT.Copy).then_inc(h_hi_ready, 1)

            act.wait_ge(kT_ready, 1)
            for rows in (half_rows(0), half_rows(1)):
                activation(kT_hi[0][rows, :, :, :], kT[half_rows(0), :, :, :], ACT.Copy).then_inc(kT_hi_ready, 1)
            x_hi(0)
            context_out()
            act.wait_ge(kT_hi_ready, 4)
            keys_high(0, range(POOL_HI_HEAD))
            act.wait_ge(wq_loaded, 32)
            q_hi(0)
            keys_high(1, range(HG))
            act.wait_ge(consts_loaded, 16 * 4)
            activation(gate[:, :], gates[:, :], ACT.Tanh).then_inc(gate_ready, 1)
            values_out(0)
            exps(0, 0)
            values_out(1)
            exps(0, 1)
            prob_out(0, 0)
            prob_out(0, 1)
            exps(0, 2)
            prob_out(0, 2)
            exps(0, 3)
            prob_out(0, 3)
            o_hi(0)
            x_hi(1)
            q_hi(1)
            f_hi(0)

            def iteration(e, g, more):
                nc.scalar.preload_act_table(ACT.Gelu)
                for f in range(FC):
                    gelu(e, f)
                    h_hi(e, f)
                nc.scalar.preload_act_table(ACT.Exp)
                exps(g, 0)
                exps(g, 1)
                prob_out(g, 0)
                prob_out(g, 1)
                exps(g, 2)
                prob_out(g, 2)
                exps(g, 3)
                prob_out(g, 3)
                o_hi(g)
                if more:
                    x_hi(g + 1)
                    q_hi(g + 1)
                f_hi(g)

            with act.Fori(0, E - 2) as i:
                iteration(i, i + 1, True)
            iteration(E - 2, E - 1, False)
            nc.scalar.preload_act_table(ACT.Gelu)
            for f in range(FC):
                gelu(E - 1, f)
                h_hi(E - 1, f)

        @block.vector
        def _(dve):
            v = nc.vector
            self_count = [0]

            def done(ins):
                self_count[0] += 1
                ins.then_inc(dve_self, 1)
                dve.wait_ge(dve_self, self_count[0])

            dve.sem_inc(final_done, B)
            dve.wait_ge(mask_loaded, 48)
            v.tensor_scalar(mcol[:, :], mcol_i[:, :], 0.0, None, ALU.not_equal).then_inc(mask_ready, 1)
            done(v.tensor_scalar(mrow, mrow_i[:, :], 0.0, None, ALU.not_equal))
            dve.wait_ge(pool_const, 6)
            dve.wait_ge(mask_ready, 1)
            done(v.tensor_tensor(gdiag, ident[0:K, 0:K], mrow, ALU.mult))
            dve.wait_ge(count_ps_ready, 1)
            done(v.scalar_tensor_tensor(first[:, :], attn_ps[0][0:K, 0:1], 1.0, mcol[0:K, :], ALU.is_equal, ALU.mult))
            v.scalar_tensor_tensor(wcol[:, :], attn_ps[1][:, 0:1], 0.0, mcol[:, :], ALU.is_equal, ALU.add).then_inc(wcol_ready, 1)
            done(v.tensor_scalar(mrow, mrow, -1.0, 1.0, ALU.mult, ALU.add))
            v.scalar_tensor_tensor(gsel, mrow, first[:, 0:1], gdiag, ALU.mult, ALU.add).then_inc(gsel_ready, 1)

            def stats(g, n):
                xg = group(g)
                halves = [(half * 2, half * 2 + 1) for half in range(2)]
                for half, tiles in enumerate(halves):
                    if n == 1:
                        dve.wait_ge(x1_ready, g * 2 + half + 1)
                    alone(dve)
                    for t in tiles:
                        last = v.bn_stats(stat6[:, t, :], xg[:, t, :])
                    last.then_inc(stats_done[n], 1)
                for half, tiles in enumerate(halves):
                    dve.wait_ge(stats_done[n], g * 4 + half + 1)
                    alone(dve)
                    for t in tiles:
                        last = v.bn_aggr(stat2[:, n, t, :], stat6[:, t, :])
                    last.then_inc(stats_done[n], 1)
                    dve.wait_ge(stats_done[n], g * 4 + half + 3)
                    v.tensor_scalar(var_eps[:, n, half * 2:half * 2 + 2], stat2[:, n, half * 2:half * 2 + 2, 1], EPS, None,
                                    ALU.add).then_inc((ln1_var, ln2_var)[n], 1)

            def scaled(g, n):
                xg = group(g)
                for t in range(B):
                    if t % 2 == 0:
                        dve.wait_ge((rstd1_ready, rstd2_ready)[n], g * 2 + t // 2 + 1)
                    v.tensor_scalar(norm[:, t, :], xg[:, t, :], stat2[:, n, t, 0:1], rstd[:, n, t:t + 1],
                                    ALU.subtract, ALU.mult).then_inc((xn_ready, x1n_ready)[n], 1)

            stats_done = [sem("stats1_done"), sem("stats2_done")]

            def lo_part(lo, hi, ps, hi_ready, signal, g):
                for c in range(C):
                    dve.wait_ge(hi_ready, g * C + c + 1)
                    v.tensor_tensor(lo[:, c, :], ps[c][:, :], hi[:, c, :].bitcast(F32), ALU.subtract).then_inc(signal, 1)

            def q_lo(g, parts):
                for part in parts:
                    c, side = part // 2, part % 2
                    dve.wait_ge(q_hi_ready, g * (C * 2) + part + 1)
                    rows = half_rows(side)
                    v.scalar_tensor_tensor(qT[half_rows(1 - side), part, :], score_ps[c][rows, :],
                                           bq_sb[rows, c:c + 1], qT[rows, part, :].bitcast(F32),
                                           ALU.add, ALU.subtract).then_inc(q_ready, 1)

            max_done = sem("max_done")
            rden_done = sem("rden_done")

            def maxima(g, t, bank=score_ps):
                for c in range(C):
                    dve.wait_ge(s_ps_ready, g * (B * C) + t * C + c + 1)
                    v.tensor_reduce(smax[:, t % 2, c * HG:(c + 1) * HG],
                                    bank[c][:, :].rearrange("p (h k) -> p h k", k=K), AX_X, ALU.max).then_inc(max_done, 1)

            def shift(g, t, bank=score_ps):
                if t >= 2:
                    dve.wait_ge(pT_ps_ready, g * (B * C) + (t - 1) * C)
                for c in range(C):
                    dve.wait_ge(max_done, g * (B * C) + t * C + c + 1)
                    v.tensor_tensor(prob[:, t % 2, c * TOK:(c + 1) * TOK].rearrange("p (h k) -> p h k", k=K),
                                    bank[c][:, :].rearrange("p (h k) -> p h k", k=K),
                                    smax[:, t % 2, c * HG:(c + 1) * HG].unsqueeze(2).to_broadcast([P, HG, K]),
                                    ALU.subtract).then_inc(shifted, 1)

            def normalise(g, t):
                if t >= 2:
                    dve.wait_ge(o_ready, g * B + t - 1)
                dve.wait_ge(pv_ready, g * B + t + 1)
                pairs = attn_ps[t % 2][:, 0:PAIRS * PW].rearrange("p (j n) -> p j n", n=PW)
                v.reciprocal(rden[:, t % 2, :].rearrange("p (j a) -> p j a", a=2), pairs[:, :, 2 * HD:PW]).then_inc(rden_done, 1)
                dve.wait_ge(rden_done, g * B + t + 1)
                v.tensor_tensor(attn[:, t, :].rearrange("p (j a d) -> p j a d", a=2, d=HD),
                                pairs[:, :, 0:2 * HD].rearrange("p j (a d) -> p j a d", a=2),
                                rden[:, t % 2, :].rearrange("p (j a) -> p j a", a=2).unsqueeze(3).to_broadcast([P, PAIRS, 2, HD]),
                                ALU.mult).then_inc(o_ready, 1)

            def residual(g):
                dve.wait_ge(xb_ready, g + 1)
                xg = group(g).rearrange("p (h b) d -> p h (b d)", h=2)
                for n in range(2):
                    dve.wait_ge(wo_ps_ready, g * 2 + n + 1)
                    v.scalar_tensor_tensor(xg[:, n, :], score_ps[n][:, :], gate[:, 0:1], xg[:, n, :],
                                           ALU.mult, ALU.add).then_inc(x1_ready, 1)
                stats(g, 1)

            def h_lo(e, f):
                dve.wait_ge(h_hi_ready, e * FC + f + 1)
                v.tensor_tensor(hT_lo[:, f, :], hid[:, f % 2, :], hT_hi[:, f, :].bitcast(F32), ALU.subtract).then_inc(h_ready, 1)

            def final(e, t, banks=y_ps):
                if t == 0:
                    dve.wait_ge(x1b_ready, e + 1)
                dve.wait_ge(y_ps_ready, e * B + t + 1)
                xg = group(e)
                v.scalar_tensor_tensor(xg[:, t, :], banks[t], gate[:, 1:2], xg[:, t, :],
                                       ALU.mult, ALU.add).then_inc(final_done, 1)

            def x_scaled(g):
                scaled(g, 0)

            def x_lo(g):
                lo_part(xT_lo, xT_hi, attn_ps, xT_hi_ready, xT_ready, g)

            def o_lo(g):
                lo_part(oT_lo, oT_hi, trans_ps, oT_hi_ready, oT_ready, g)

            def f_lo(g):
                lo_part(fT_lo, fT_hi, trans_ps, fT_hi_ready, fT_ready, g)

            dve.wait_ge(x0_loaded, 16)
            stats(0, 0)
            scaled(0, 0)
            dve.wait_ge(vals_zero, 2)
            dve.wait_ge(wcol_ready, 1)
            for side in range(2):
                rows = slice(side * K, (side + 1) * K)
                dst = vals[rows, :, 0:PAIRS * PW].rearrange("p b (j n) -> p b j n", n=PW)
                last = v.tensor_scalar(dst[:, :, :, 2 * HD + side], ones[rows, 0:B * PAIRS].rearrange("p (b j) -> p b j", b=B),
                                       wcol[rows, 0:1], None, ALU.mult)
            last.then_inc(vals_ones_ready, 1)
            dve.wait_ge(wv_loaded, 32)
            for side in range(2):
                rows, cols = slice(side * K, (side + 1) * K), slice(side * HD, (side + 1) * HD)
                dst, src = (a[rows, :].rearrange("p (j n) -> p j n", n=2 * HD)[:, :, cols] for a in (bv_w, bv_sb))
                last = v.tensor_scalar(dst, src, wcol[rows, 0:1], None, ALU.mult)
            last.then_inc(bv_ready, 1)
            dve.wait_ge(wk_loaded, 32)
            for c in range(C):
                dve.wait_ge(kv_ps_ready, c + 1)
                last = v.tensor_scalar(kT[:, c, :, :], hid_ps[c][:, 0:B * K].rearrange("p (b k) -> p b k", b=B),
                                       bk_sb[:, c:c + 1], SCALE, ALU.add, ALU.mult)
            last.then_inc(kT_ready, 1)
            dve.wait_ge(kT_ready, 1)
            for rows in (half_rows(1), half_rows(0)):
                v.tensor_scalar(kT_hi[1][rows, :, :, :], kT[half_rows(1), :, :, :], 1.0, None, ALU.mult).then_inc(kT_hi_ready, 1)
            dve.wait_ge(kT_hi_ready, 4)
            for side in range(2):
                rows = half_rows(side)
                last = v.tensor_tensor(kT_lo[rows, :, :, :], kT[rows, :, :, :], kT_hi[side][rows, :, :, :].bitcast(F32),
                                       ALU.subtract)
            last.then_inc(kT_lo_ready, 1)
            x_lo(0)
            dve.wait_ge(kT_lo_ready, 1)
            for h in range(POOL_LO_HEAD):
                last = v.tensor_scalar(*keys_lo_part(0, h), None, ALU.mult)
            last.then_inc(keys_lo_ready, 1)
            dve.wait_ge(wq_loaded, 32)
            q_lo(0, range(4))
            maxima(0, 0)
            shift(0, 0)
            maxima(0, 1, hid_ps)
            dve.wait_ge(kv_ps_ready, C + 2)
            dve.wait_ge(wo_ready, 1)
            shift(0, 1, hid_ps)
            maxima(0, 2)
            shift(0, 2)
            maxima(0, 3, hid_ps)
            shift(0, 3, hid_ps)
            normalise(0, 0)
            dve.wait_ge(gate_ready, 1)
            v.tensor_scalar(bo_g[:, :], bo_sb, gate[:, 0:1], None, ALU.mult).then_inc(bo_ready, 1)
            dve.wait_ge(x1_loaded, 16)
            stats(1, 0)
            normalise(0, 1)
            dve.wait_ge(bo_ready, 1)
            normalise(0, 2)
            x_scaled(1)
            normalise(0, 3)
            o_lo(0)
            x_lo(1)
            residual(0)
            scaled(0, 1)
            q_lo(1, range(1))
            f_lo(0)
            q_lo(1, range(1, 4))
            dve.wait_ge(x_loaded, 16)

            def iteration(e, g, more):
                h_lo(e, 0)
                h_lo(e, 1)
                maxima(g, 0)
                shift(g, 0)
                h_lo(e, 2)
                h_lo(e, 3)
                maxima(g, 1)
                h_lo(e, 4)
                shift(g, 1)
                h_lo(e, 5)
                h_lo(e, 6)
                h_lo(e, 7)
                final(e, 0)
                maxima(g, 2)
                shift(g, 2)
                normalise(g, 0)
                maxima(g, 3)
                shift(g, 3)
                if more:
                    stats(g + 1, 0)
                normalise(g, 1)
                normalise(g, 2)
                if more:
                    x_scaled(g + 1)
                final(e, 1)
                normalise(g, 3)
                o_lo(g)
                if more:
                    x_lo(g + 1)
                residual(g)
                final(e, 2)
                scaled(g, 1)
                if more:
                    q_lo(g + 1, range(1))
                f_lo(g)
                final(e, 3)
                if more:
                    q_lo(g + 1, range(1, 4))

            with dve.Fori(0, E - 2) as i:
                iteration(i, i + 1, True)
            iteration(E - 2, E - 1, False)
            for f in range(FC):
                h_lo(E - 1, f)
            for t in range(B):
                final(E - 1, t, y_last_ps)


def kernel(x, ctx_1024, mask_1xS2_if1, g_xattn, g_ffn, L0_xattn_Wq, L0_xattn_bq, L0_xattn_Wk, L0_xattn_bk,
           L0_xattn_Wv, L0_xattn_bv, L0_xattn_Wo, L0_xattn_bo, L0_ffn_w1, L0_ffn_b1, L0_ffn_w2, L0_ffn_b2):
    import numpy as np
    import concourse.bacc as bacc
    from concourse.bass_utils import run_bass_kernel_spmd

    def halves(w):
        return np.ascontiguousarray(np.asarray(w).reshape(C, P, -1).transpose(1, 0, 2))

    def column(b):
        return np.ascontiguousarray(np.asarray(b).reshape(C, P).T)

    def row(b):
        return np.ascontiguousarray(np.asarray(b).reshape(1, -1))

    arrays = {
        "x": np.ascontiguousarray(np.asarray(x).reshape(B, E, P, D).transpose(1, 2, 0, 3)).reshape(E, P, B * D),
        "ctx": np.ascontiguousarray(np.asarray(ctx_1024).transpose(1, 0, 2)),
        "mask": np.ascontiguousarray(np.asarray(mask_1xS2_if1)),
        "g_x": row(g_xattn), "g_f": row(g_ffn),
        "wq": halves(L0_xattn_Wq), "bq": column(L0_xattn_bq),
        "wk": halves(L0_xattn_Wk), "bk": column(L0_xattn_bk),
        "wv": halves(L0_xattn_Wv), "bv": row(L0_xattn_bv),
        "wo": halves(L0_xattn_Wo), "bo": row(L0_xattn_bo),
        "w1": np.ascontiguousarray(np.asarray(L0_ffn_w1).reshape(E, F, C, P).transpose(0, 3, 2, 1)).reshape(E, P, C * F),
        "b1": np.ascontiguousarray(np.asarray(L0_ffn_b1).reshape(E, FC, P).transpose(2, 0, 1)),
        "w2": np.ascontiguousarray(np.asarray(L0_ffn_w2).reshape(E, D, FC, P).transpose(0, 3, 2, 1)).reshape(E, P, FC * D),
        "b2": np.ascontiguousarray(np.asarray(L0_ffn_b2)),
    }
    nc = bacc.Bacc("TRN2", target_bir_lowering=False, num_devices=1)
    feeds = {f"in_{n}": a for n, a in arrays.items()}
    args = [nc.dram_tensor(n, a.shape, mybir.dt.from_np(a.dtype), kind="ExternalInput").ap() for n, a in feeds.items()]
    out = nc.dram_tensor("out", (E, P, B * D), F32, kind="ExternalOutput").ap()
    build(nc, *args, out)
    r = run_bass_kernel_spmd(nc, [feeds], core_ids=[0])
    got = r.results[0]["out"].reshape(E, P, B, D).transpose(2, 0, 1, 3).reshape(B, S, D)
    return np.ascontiguousarray(got)
```
